# Optimizing a Trainium2 kernel written in Bass

```python
import numpy as np
import jax
import jax.numpy as jnp

def _softmax(x, axis=-1):
    return jax.nn.softmax(x, axis=axis)

def _gelu(x):
    return jax.nn.gelu(x, approximate=True)

def _silu(x):
    return jax.nn.silu(x)

def _sigmoid(x):
    return jax.nn.sigmoid(x)

def _layernorm(x, axis=-1, eps=1e-05):
    m = jnp.mean(x, axis=axis, keepdims=True)
    v = jnp.var(x, axis=axis, keepdims=True)
    return (x - m) / jnp.sqrt(v + eps)

def _scatter_add(tgt, idx, src, axis=0):
    return tgt.at[idx].add(src)

def _segment_sum(src, seg, n):
    return jax.ops.segment_sum(src, seg, n)
kernel_name = 'mk_conv_attn_hybrid_d2_conv_nchw256_r2_1ec99b'

def setup_inputs(seed: int=0):
    np.random.seed(seed)
    _w = jnp.asarray

    def _rec_inputs():
        import jax
        import jax.numpy as jnp
        _gk = jax.random.key(seed)
        x = 7.22e-05 + 1 * jax.random.normal(jax.random.fold_in(_gk, 1), (32, 128, 32, 32), jnp.float32)
        return x
    x = _rec_inputs()

    def _L0_conv_setup():
        import jax, jax.numpy as jnp
        import numpy as np
        B, C, H, W = (32, 128, 32, 32)
        key = jax.random.key(seed)
        ks = jax.random.split(key, 7)
        s = 1.0 / np.sqrt(C)
        return {'x': jax.random.normal(ks[0], (B, C, H, W), dtype=jnp.float32), 'Wq': jax.random.normal(ks[1], (C, C), dtype=jnp.float32) * s, 'bq': jax.random.normal(ks[2], (C,), dtype=jnp.float32) * 0.01, 'Wk': jax.random.normal(ks[3], (C, C), dtype=jnp.float32) * s, 'bk': jax.random.normal(ks[4], (C,), dtype=jnp.float32) * 0.01, 'Wv': jax.random.normal(ks[5], (C, C), dtype=jnp.float32) * s, 'bv': jax.random.normal(ks[6], (C,), dtype=jnp.float32) * 0.01}
    _L0_conv_all = _L0_conv_setup()
    _L0_conv_in = {k: v for k, v in _L0_conv_all.items() if k in ('Wq', 'bq', 'Wk', 'bk', 'Wv', 'bv')}
    del _L0_conv_all

    def _L1_attn_setup():
        import jax, jax.numpy as jnp
        import numpy as np
        B, L, D = (4, 1024, 128)
        DI, DS, DR, K = (256, 16, 16, 4)

        def _mamba(x, in_proj_w, conv_w, conv_b, x_proj_w, dt_proj_w, dt_proj_b, A_log, Dp, out_proj_w):
            Bsz, Ls, _ = x.shape
            xz = jnp.einsum('bld,ed->ble', x, in_proj_w)
            xc, z = jnp.split(xz, 2, axis=-1)
            xp = jnp.pad(xc, ((0, 0), (K - 1, 0), (0, 0)))
            xc = sum((xp[:, k:k + Ls, :] * conv_w[:, k] for k in range(K))) + conv_b
            xc = jax.nn.silu(xc)
            x_dbl = jnp.einsum('bld,ed->ble', xc, x_proj_w)
            dt = x_dbl[..., :DR]
            Bm = x_dbl[..., DR:DR + DS]
            Cm = x_dbl[..., DR + DS:]
            dt = jax.nn.softplus(jnp.einsum('blr,dr->bld', dt, dt_proj_w) + dt_proj_b)
            A = -jnp.exp(A_log)
            dA = jnp.exp(dt[..., None] * A)
            dBx = dt[..., None] * Bm[:, :, None, :] * xc[..., None]

            def step(h, inp):
                dA_t, dBx_t, C_t = inp
                h = dA_t * h + dBx_t
                y = jnp.einsum('bds,bs->bd', h, C_t)
                return (h, y)
            h0 = jnp.zeros((Bsz, DI, DS), x.dtype)
            _, ys = jax.lax.scan(step, h0, (dA.transpose(1, 0, 2, 3), dBx.transpose(1, 0, 2, 3), Cm.transpose(1, 0, 2)))
            y = ys.transpose(1, 0, 2) + xc * Dp
            y = y * jax.nn.silu(z)
            return jnp.einsum('bld,ed->ble', y, out_proj_w)
        key = jax.random.key(seed)
        ks = jax.random.split(key, 16)
        n = lambda k, s, sc=0.02: jax.random.normal(k, s, dtype=jnp.float32) * sc
        return {'x': jax.random.normal(ks[0], (B, L, D), dtype=jnp.float32), 'in_proj_w': n(ks[1], (2, 2 * DI, D)), 'conv_w': n(ks[2], (2, DI, K), 0.2), 'conv_b': n(ks[3], (2, DI)), 'x_proj_w': n(ks[4], (2, DR + 2 * DS, DI)), 'dt_proj_w': n(ks[5], (2, DI, DR), 0.1), 'dt_proj_b': n(ks[6], (2, DI)), 'A_log': jax.random.uniform(ks[7], (2, DI, DS), dtype=jnp.float32), 'Dp': n(ks[8], (2, DI), 1.0), 'out_proj_w': n(ks[9], (2, D, DI)), 'ln_g': jnp.ones((D,), jnp.float32), 'ln_b': jnp.zeros((D,), jnp.float32), 'w1': n(ks[10], (2 * D, D)), 'b1': jnp.zeros((2 * D,), jnp.float32), 'w2': n(ks[11], (D, 2 * D)), 'b2': jnp.zeros((D,), jnp.float32)}
    _L1_attn_all = _L1_attn_setup()
    _L1_attn_in = {k: v for k, v in _L1_attn_all.items() if k in ('in_proj_w', 'conv_w', 'conv_b', 'x_proj_w', 'dt_proj_w', 'dt_proj_b', 'A_log', 'Dp', 'out_proj_w', 'ln_g', 'ln_b', 'w1', 'b1', 'w2', 'b2')}
    del _L1_attn_all

    def _L1_ffn_setup():
        import jax, jax.numpy as jnp
        import numpy as np
        B, S, D = (8, 2048, 128)
        H = 4 * D
        CAPACITY = 0.5
        key = jax.random.key(seed)
        ks = jax.random.split(key, 6)
        x = jax.random.normal(ks[0], (B, S, D), dtype=jnp.float32)
        attention_mask = jnp.zeros((B, 1, 1, S), dtype=jnp.float32)
        wr = jax.random.normal(ks[1], (D, 1), dtype=jnp.float32) * 0.02
        br = jnp.zeros((1,), dtype=jnp.float32)
        w1 = jax.random.normal(ks[2], (D, H), dtype=jnp.float32) * 0.02
        b1 = jnp.zeros((H,), dtype=jnp.float32)
        w2 = jax.random.normal(ks[3], (H, D), dtype=jnp.float32) * 0.02
        b2 = jnp.zeros((D,), dtype=jnp.float32)
        return {'x': x, 'attention_mask': attention_mask, 'wr': wr, 'br': br, 'w1': w1, 'b1': b1, 'w2': w2, 'b2': b2}
    _L1_ffn_all = _L1_ffn_setup()
    _L1_ffn_in = {k: v for k, v in _L1_ffn_all.items() if k in ('attention_mask', 'wr', 'br', 'w1', 'b1', 'w2', 'b2')}
    del _L1_ffn_all
    return {'x': x, 'L0_conv_Wq': _L0_conv_in['Wq'], 'L0_conv_bq': _L0_conv_in['bq'], 'L0_conv_Wk': _L0_conv_in['Wk'], 'L0_conv_bk': _L0_conv_in['bk'], 'L0_conv_Wv': _L0_conv_in['Wv'], 'L0_conv_bv': _L0_conv_in['bv'], 'L1_attn_in_proj_w': _L1_attn_in['in_proj_w'], 'L1_attn_conv_w': _L1_attn_in['conv_w'], 'L1_attn_conv_b': _L1_attn_in['conv_b'], 'L1_attn_x_proj_w': _L1_attn_in['x_proj_w'], 'L1_attn_dt_proj_w': _L1_attn_in['dt_proj_w'], 'L1_attn_dt_proj_b': _L1_attn_in['dt_proj_b'], 'L1_attn_A_log': _L1_attn_in['A_log'], 'L1_attn_Dp': _L1_attn_in['Dp'], 'L1_attn_out_proj_w': _L1_attn_in['out_proj_w'], 'L1_attn_ln_g': _L1_attn_in['ln_g'], 'L1_attn_ln_b': _L1_attn_in['ln_b'], 'L1_attn_w1': _L1_attn_in['w1'], 'L1_attn_b1': _L1_attn_in['b1'], 'L1_attn_w2': _L1_attn_in['w2'], 'L1_attn_b2': _L1_attn_in['b2'], 'L1_ffn_attention_mask': _L1_ffn_in['attention_mask'], 'L1_ffn_wr': _L1_ffn_in['wr'], 'L1_ffn_br': _L1_ffn_in['br'], 'L1_ffn_w1': _L1_ffn_in['w1'], 'L1_ffn_b1': _L1_ffn_in['b1'], 'L1_ffn_w2': _L1_ffn_in['w2'], 'L1_ffn_b2': _L1_ffn_in['b2']}

def reference(x, L0_conv_Wq, L0_conv_bq, L0_conv_Wk, L0_conv_bk, L0_conv_Wv, L0_conv_bv, L1_attn_in_proj_w, L1_attn_conv_w, L1_attn_conv_b, L1_attn_x_proj_w, L1_attn_dt_proj_w, L1_attn_dt_proj_b, L1_attn_A_log, L1_attn_Dp, L1_attn_out_proj_w, L1_attn_ln_g, L1_attn_ln_b, L1_attn_w1, L1_attn_b1, L1_attn_w2, L1_attn_b2, L1_ffn_attention_mask, L1_ffn_wr, L1_ffn_br, L1_ffn_w1, L1_ffn_b1, L1_ffn_w2, L1_ffn_b2):
    import jax
    import jax.numpy as jnp

    def _L0_conv_ref(x, Wq, bq, Wk, bk, Wv, bv):
        import jax, jax.numpy as jnp
        import numpy as np
        B, C, H, W = (32, 128, 32, 32)
        b, c, h, w = x.shape
        xf = x.reshape(b, c, h * w)
        Q = jnp.einsum('oc,bcn->bon', Wq, xf) + bq[:, None]
        K = jnp.einsum('oc,bcn->bon', Wk, xf) + bk[:, None]
        V = jnp.einsum('oc,bcn->bon', Wv, xf) + bv[:, None]
        scale = 1.0 / jnp.sqrt(jnp.asarray(c, dtype=x.dtype))
        attn = jnp.einsum('bcn,bcm->bnm', Q, K) * scale
        attn = jax.nn.softmax(attn, axis=-1)
        out = jnp.einsum('bnm,bcm->bcn', attn, V)
        return out.reshape(b, c, h, w) + x

    def _L1_attn_ref(x, in_proj_w, conv_w, conv_b, x_proj_w, dt_proj_w, dt_proj_b, A_log, Dp, out_proj_w, ln_g, ln_b, w1, b1, w2, b2):
        import jax, jax.numpy as jnp
        import numpy as np
        B, L, D = (4, 1024, 128)
        DI, DS, DR, K = (256, 16, 16, 4)

        def _mamba(x, in_proj_w, conv_w, conv_b, x_proj_w, dt_proj_w, dt_proj_b, A_log, Dp, out_proj_w):
            Bsz, Ls, _ = x.shape
            xz = jnp.einsum('bld,ed->ble', x, in_proj_w)
            xc, z = jnp.split(xz, 2, axis=-1)
            xp = jnp.pad(xc, ((0, 0), (K - 1, 0), (0, 0)))
            xc = sum((xp[:, k:k + Ls, :] * conv_w[:, k] for k in range(K))) + conv_b
            xc = jax.nn.silu(xc)
            x_dbl = jnp.einsum('bld,ed->ble', xc, x_proj_w)
            dt = x_dbl[..., :DR]
            Bm = x_dbl[..., DR:DR + DS]
            Cm = x_dbl[..., DR + DS:]
            dt = jax.nn.softplus(jnp.einsum('blr,dr->bld', dt, dt_proj_w) + dt_proj_b)
            A = -jnp.exp(A_log)
            dA = jnp.exp(dt[..., None] * A)
            dBx = dt[..., None] * Bm[:, :, None, :] * xc[..., None]

            def step(h, inp):
                dA_t, dBx_t, C_t = inp
                h = dA_t * h + dBx_t
                y = jnp.einsum('bds,bs->bd', h, C_t)
                return (h, y)
            h0 = jnp.zeros((Bsz, DI, DS), x.dtype)
            _, ys = jax.lax.scan(step, h0, (dA.transpose(1, 0, 2, 3), dBx.transpose(1, 0, 2, 3), Cm.transpose(1, 0, 2)))
            y = ys.transpose(1, 0, 2) + xc * Dp
            y = y * jax.nn.silu(z)
            return jnp.einsum('bld,ed->ble', y, out_proj_w)
        fwd = _mamba(x, in_proj_w[0], conv_w[0], conv_b[0], x_proj_w[0], dt_proj_w[0], dt_proj_b[0], A_log[0], Dp[0], out_proj_w[0])
        bwd = _mamba(x[:, ::-1, :], in_proj_w[1], conv_w[1], conv_b[1], x_proj_w[1], dt_proj_w[1], dt_proj_b[1], A_log[1], Dp[1], out_proj_w[1])
        m = fwd + bwd
        mu = jnp.mean(m, axis=-1, keepdims=True)
        var = jnp.mean(jnp.square(m - mu), axis=-1, keepdims=True)
        h = (m - mu) / jnp.sqrt(var + 1e-05) * ln_g + ln_b
        p = jax.nn.leaky_relu(h @ w1.T + b1, negative_slope=0.01) @ w2.T + b2
        return m + p

    def _L1_ffn_ref(x, attention_mask, wr, br, w1, b1, w2, b2):
        import jax, jax.numpy as jnp
        import numpy as np
        B, S, D = (8, 2048, 128)
        H = 4 * D
        CAPACITY = 0.5
        b, s, d = x.shape
        weights = (jnp.einsum('bsd,do->bso', x, wr) + br)[..., 0]
        k = max(1, int(CAPACITY * s))
        kk = k - 1 if k > 1 else 1
        _, idx = jax.lax.top_k(weights, k)
        sel_idx = idx[:, :kk]
        sel = jnp.take_along_axis(x, sel_idx[:, :, None], axis=1)
        h = jax.nn.gelu(jnp.einsum('bkd,dh->bkh', sel, w1) + b1)
        y = jnp.einsum('bkh,hd->bkd', h, w2) + b2
        w_sel = jnp.take_along_axis(weights, sel_idx, axis=1)
        y = y * w_sel[..., None]
        batch_idx = jnp.arange(b)[:, None]
        processed = jnp.zeros_like(x).at[batch_idx, sel_idx].set(y)
        return processed + x

    def _gn(v, G=32, eps=1e-05):
        B_, C_, H_, W_ = v.shape
        g = v.reshape(B_, G, C_ // G, H_, W_)
        m = jnp.mean(g, axis=(2, 3, 4), keepdims=True)
        s = jnp.var(g, axis=(2, 3, 4), keepdims=True)
        return ((g - m) / jnp.sqrt(s + eps)).reshape(v.shape)

    def _ln_c(v, eps=1e-06):
        m = jnp.mean(v, axis=1, keepdims=True)
        s = jnp.var(v, axis=1, keepdims=True)
        return (v - m) / jnp.sqrt(s + eps)

    def _ln_t(v, eps=1e-05):
        m = jnp.mean(v, axis=-1, keepdims=True)
        s = jnp.var(v, axis=-1, keepdims=True)
        return (v - m) / jnp.sqrt(s + eps)

    def _to_tokens(v):
        B_, C_, H_, W_ = v.shape
        return v.reshape(B_, C_, H_ * W_).transpose(0, 2, 1)

    def _from_tokens(t, like):
        B_, C_, H_, W_ = like.shape
        return t.transpose(0, 2, 1).reshape(B_, C_, H_, W_)
    x = _L0_conv_ref(x, L0_conv_Wq, L0_conv_bq, L0_conv_Wk, L0_conv_bk, L0_conv_Wv, L0_conv_bv)
    t = _to_tokens(x)
    t = t + _L1_attn_ref(_ln_t(t), L1_attn_in_proj_w, L1_attn_conv_w, L1_attn_conv_b, L1_attn_x_proj_w, L1_attn_dt_proj_w, L1_attn_dt_proj_b, L1_attn_A_log, L1_attn_Dp, L1_attn_out_proj_w, L1_attn_ln_g, L1_attn_ln_b, L1_attn_w1, L1_attn_b1, L1_attn_w2, L1_attn_b2)
    t = t + _L1_ffn_ref(_ln_t(t), L1_ffn_attention_mask, L1_ffn_wr, L1_ffn_br, L1_ffn_w1, L1_ffn_b1, L1_ffn_w2, L1_ffn_b2)
    x = _from_tokens(t, x)
    return x

_drawn_inputs = setup_inputs


def setup_inputs(seed=0):
    import zlib

    import numpy as np

    out = dict(_drawn_inputs(seed))
    spreads = {'L1_attn_ln_g': (1.0, 0.6),
     'L1_attn_ln_b': (0.0, 0.8),
     'L1_attn_b1': (0.0, 0.388),
     'L1_attn_b2': (0.0, 0.1),
     'L1_ffn_b1': (0.0, 0.8),
     'L1_ffn_b2': (0.0, 0.8)}
    factors = {'L0_conv_bq': 23.698,
     'L0_conv_bk': 64.0,
     'L0_conv_bv': 5.345,
     'L1_attn_conv_b': 8.0,
     'L1_attn_x_proj_w': 8.0,
     'L1_attn_dt_proj_w': 25.846,
     'L1_attn_dt_proj_b': 57.814,
     'L1_attn_A_log': 47.637,
     'L1_ffn_wr': 7.686,
     'L1_ffn_w1': 8.0,
     'L1_ffn_w2': 8.0}
    for name, (base, spread) in spreads.items():
        noise = np.random.default_rng([zlib.crc32(name.encode()), seed]).standard_normal(out[name].shape)
        drawn = base * np.exp(spread * noise) if base else spread * noise
        out[name] = jnp.asarray(drawn.astype(out[name].dtype))
    for name, factor in factors.items():
        out[name] = (out[name] * factor).astype(out[name].dtype)
    return out
```

```python
import concourse.bass as bass
from concourse import mybir
from contextlib import ExitStack
import numpy as np

def conv_attn_mamba_mod_kernel(nc, I, out):
    fp32 = mybir.dt.float32
    ALU = mybir.AluOpType
    ACT = mybir.ActivationFunctionType
    AX = mybir.AxisListType

    B, C, T = I["x"].shape

    P = 128
    NB = T // P
    BANK = 512
    NCH = T // BANK
    QB = BANK // P
    DIRS, DI, KCONV = I["conv_w"].shape
    NH = DI // P
    DS = I["A_log"].shape[2]
    DR = I["dt_proj_w"].shape[2]
    HM = I["w1"].shape[1] // P
    HF = I["f_w1"].shape[1] // P
    PAD = KCONV - 1
    KEPT = T // 2 - 1
    SCALE = float(np.float32(1.0) / np.sqrt(np.float32(C)))
    EPS = 1e-5
    SLOPE = 0.01
    EXP_MAX = 1e15
    STEPS = DS * NCH
    RING = 3

    ctx = ExitStack()
    with ctx:
        def sb(name, shape):
            return ctx.enter_context(nc.sbuf_tensor(name, shape, fp32))

        first_sem = []

        def sem(name):
            s = ctx.enter_context(nc.semaphore(name))
            first_sem.append(s)
            return s

        ident = sb("ident", [P, P])
        below = sb("below", [P, P])
        ones_row = sb("ones_row", [1, P])
        wq = sb("wq", [C, C])
        wk = sb("wk", [C, C])
        wv = sb("wv", [C, C])
        bq = sb("bq", [C, 1])
        bk = sb("bk", [C, 1])
        bv_rows = sb("bv_rows", [P, C])
        w_in = sb("w_in", [C, DIRS, 2 * DI])
        cw_rows = sb("cw_rows", [P, DIRS, KCONV, DI])
        conv_b = sb("conv_b", [P, DIRS, NH])
        w_x = sb("w_x", [P, DIRS, NH, DR + 2 * DS])
        w_dt = sb("w_dt", [DR, DIRS, DI])
        b_dt = sb("b_dt", [P, DIRS, NH])
        a_neg = sb("a_neg", [P, DIRS, NH, DS])
        d_skip = sb("d_skip", [P, DIRS, NH])
        w_out = sb("w_out", [P, DIRS, NH, C])
        ln_g = sb("ln_g", [C, 1])
        ln_b = sb("ln_b", [C, 1])
        w1 = sb("w1", [C, HM * P])
        b1 = sb("b1", [P, HM])
        w2 = sb("w2", [P, HM, C])
        b2 = sb("b2", [1, C])
        wr = sb("wr", [C, 1])
        wr_cols = sb("wr_cols", [C, P])
        br = sb("br", [P, 1])
        f_w1 = sb("f_w1", [C, HF * P])
        f_b1 = sb("f_b1", [P, HF])
        f_w2 = sb("f_w2", [P, HF, C])
        f_b2 = sb("f_b2", [1, C])
        minus_half = sb("minus_half", [P, NB])

        x_in = sb("x_in", [C, T])
        q = sb("q", [C, T])
        k = sb("k", [C, T])
        v_tok = sb("v_tok", [P, NB, C])
        x_tok = sb("x_tok", [P, NB, C])
        nmax = sb("nmax", [P, NB])
        rowsum = sb("rowsum", [P, NB])
        rinv = sb("rinv", [P, NB])
        probs_g = sb("probs_g", [P, 4, T])
        t1 = sb("t1", [P, NB, C])
        stats = sb("stats", [P, NB, 6])
        mean_var = sb("mean_var", [P, NB, 2])
        var_eps = sb("var_eps", [P, NB])
        rstd = sb("rstd", [P, NB])
        normed = sb("normed", [P, NB, C])
        x_fwd = sb("x_fwd", [C, PAD + T])
        x_bwd = sb("x_bwd", [C, PAD + T])
        xc = sb("xc", [P, NH, T])
        sz = sb("sz", [P, NH, T])
        dt16 = sb("dt16", [DR, T])
        bc = sb("bc", [P, NB, 2 * DS])
        dt = sb("dt", [P, NH, T])
        u = sb("u", [P, NH, T])
        u_tok = sb("u_tok", [P, NB, DI])
        ub = sb("ub", [P, RING, QB, DI])
        da = sb("da", [P, 2, NH, T])
        h = sb("h", [P, RING, NH, BANK])
        y_tok = u[:, :, :].rearrange("p h (b c) -> p (h b c)", c=C).rearrange("p (b d) -> p b d", d=DI)
        y = sb("y", [P, DIRS, NH, T])
        m = sz[:, 0, :].rearrange("p (b c) -> p b c", c=C)
        h1 = sz[:, 1, :]
        act1 = xc
        mt = dt[:, 0, :].rearrange("p (b c) -> p b c", c=C)
        t2 = dt[:, 1, :].rearrange("p (b c) -> p b c", c=C)
        n2 = u_tok[:, 0:4, :].rearrange("p a (b c) -> p (a b) c", c=C)
        n2c = u_tok[:, 4:8, :].rearrange("p a c -> p (a c)")
        w_row = da[:, 0, 0, :]
        junk = da[:, 0, 1, :]
        out_s = da[:, 1, 0, :]
        w_col = sb("w_col", [P, NB])
        counts = sb("counts", [P, NB, 3])
        rank = sb("rank", [P, NB])
        w_kept = sb("w_kept", [P, NB])

        ps = ctx.enter_context(nc.psum_tensor("ps", [P, 8, BANK], fp32))

        def banks(n, k):
            return ps[:, n:n + k, :].rearrange("p b c -> p (b c)")

        def blocks(n):
            return banks(n, 2).rearrange("p (b c) -> p b c", c=C)

        loaded = ctx.enter_context(nc.semaphore("loaded"))
        setup_pool = ctx.enter_context(nc.semaphore("setup_pool"))
        setup_exp = ctx.enter_context(nc.semaphore("setup_exp"))
        setup_dve = ctx.enter_context(nc.semaphore("setup_dve"))

        with nc.Block() as block:
            loads = [
                (wq[:], I["wq"]), (wk[:], I["wk"]), (wv[:], I["wv"]),
                (bq[:], I["bq"]), (bk[:], I["bk"]),
                (bv_rows[:], I["bv"].to_broadcast([P, C])),
                (w_in[:], I["in_proj"].rearrange("r c e -> c r e")),
                (cw_rows[:].rearrange("p r k e -> p (r k e)"), I["conv_rows"].to_broadcast([P, DIRS * KCONV * DI])),
                (conv_b[:], I["conv_b"]),
                (w_x[:], I["x_proj"]), (w_dt[:], I["dt_w"]), (b_dt[:], I["dt_b"]),
                (a_neg[:], I["A_logs"]), (d_skip[:], I["Dp"]), (w_out[:], I["out_w"]),
                (ln_g[:], I["ln_g"]), (ln_b[:], I["ln_b"]),
                (w1[:], I["w1"]), (b1[:], I["b1"]), (w2[:], I["w2"]), (b2[:], I["b2"]),
                (wr[:], I["wr"]), (br[:], I["br"].to_broadcast([P, 1])),
                (f_w1[:], I["f_w1"]), (f_b1[:], I["f_b1"]), (f_w2[:], I["f_w2"]), (f_b2[:], I["f_b2"]),
            ]

            @block.sync
            def _(sp):
                with nc.allow_non_contiguous_dma(reason="weights, once"):
                    for dst, src in loads:
                        sp.dma_start(dst, src).then_inc(loaded, 16)
                sp.wait_ge(loaded, 16 * len(loads))

            @block.gpsimd
            def _(pool):
                pool.memset(ident[:], 0.0).then_inc(setup_pool, 1)
                pool.memset(below[:], 1.0).then_inc(setup_pool, 1)
                pool.memset(ones_row[:], 1.0)
                pool.memset(minus_half[:], -0.5)
                pool.memset(counts[:], 0.0)
                pool.memset(x_fwd[:, 0:PAD], 0.0)
                pool.memset(x_bwd[:, 0:PAD], 0.0)
                pool.wait_ge(setup_pool, 2)
                pool.affine_select(out=ident[:], in_=ident[:], compare_op=ALU.not_equal, fill=1.0,
                                   base=0, pattern=[[-1, P]], channel_multiplier=1)
                pool.affine_select(out=below[:], in_=below[:], compare_op=ALU.is_gt, fill=0.0,
                                   base=0, pattern=[[-1, P]], channel_multiplier=1)

            @block.scalar
            def _(act):
                act.wait_ge(loaded, 16 * len(loads))
                act.activation(a_neg[:], a_neg[:], ACT.Exp).then_inc(setup_exp, 1)

            @block.vector
            def _(dve):
                dve.wait_ge(loaded, 16 * len(loads))
                dve.tensor_scalar(bq[:], bq[:], SCALE, None, ALU.mult)
                dve.tensor_copy(wr_cols[:], wr[:].to_broadcast([C, P]))
                for r in range(DIRS):
                    for tap in range(KCONV):
                        dve.tensor_tensor(cw_rows[:, r, tap, :], cw_rows[:, r, tap, :], w_in[:, r, 0:DI], ALU.mult)
                dve.wait_ge(setup_exp, 1)
                dve.tensor_scalar(a_neg[:], a_neg[:], -1.0, None, ALU.mult)

        x_loaded = sem("x_loaded")
        xt_made = sem("xt_made")
        q_made = sem("q_made")
        k_made = sem("k_made")
        v_made = sem("v_made")
        qkv_kept = sem("qkv_kept")
        xt_kept = sem("xt_kept")
        scores_made = sem("scores_made")
        max_made = sem("max_made")
        probs_made = sem("probs_made")
        probs_turned = sem("probs_turned")
        probs_kept = sem("probs_kept")
        attn_made = sem("attn_made")
        rinv_made = sem("rinv_made")
        t1_made = sem("t1_made")
        ln_stats = [sem(f"ln_stats{n}") for n in range(3)]
        ln_var = [sem(f"ln_var{n}") for n in range(3)]
        ln_eps = [sem(f"ln_eps{n}") for n in range(3)]
        ln_rstd = [sem(f"ln_rstd{n}") for n in range(3)]
        ln_made = [sem(f"ln_made{n}") for n in range(3)]
        ln_turned = [sem(f"ln_turned{n}") for n in range(3)]
        ln_kept = [sem(f"ln_kept{n}") for n in range(3)]
        xc_made = sem("xc_made")
        z_made = sem("z_made")
        xc_kept = sem("xc_kept")
        z_kept = sem("z_kept")
        dt16_made = sem("dt16_made")
        bc_made = sem("bc_made")
        dt16_kept = sem("dt16_kept")
        bc_kept = sem("bc_kept")
        dt_made = sem("dt_made")
        dt_exp = sem("dt_exp")
        dt_cut = sem("dt_cut")
        dt_log = sem("dt_log")
        dt_kept = sem("dt_kept")
        u_made = sem("u_made")
        u_turned = sem("u_turned")
        u_kept = sem("u_kept")
        ub_made = sem("ub_made")
        ub_turned = sem("ub_turned")
        da_made = sem("da_made")
        h_made = sem("h_made")
        h_turned = sem("h_turned")
        y_added = sem("y_added")
        y_turned = sem("y_turned")
        y_skip = sem("y_skip")
        y_gated = sem("y_gated")
        m_made = sem("m_made")
        m_kept = sem("m_kept")
        hid1_made = sem("hid1_made")
        hid1_kept = sem("hid1_kept")
        hid1_leaky = sem("hid1_leaky")
        mlp_made = sem("mlp_made")
        mt_made = sem("mt_made")
        t2_made = sem("t2_made")
        base_made = sem("base_made")
        w_made = sem("w_made")
        w_kept_row = sem("w_kept_row")
        w_turned = sem("w_turned")
        w_col_kept = sem("w_col_kept")
        compared = sem("compared")
        ranked = sem("ranked")
        wk_made = sem("wk_made")
        hid2_made = sem("hid2_made")
        hid2_kept = sem("hid2_kept")
        ffn_made = sem("ffn_made")
        t3_made = sem("t3_made")
        out_turned = sem("out_turned")
        out_kept = sem("out_kept")
        stored = sem("stored")

        def probs(i):
            return probs_g[:, i % 2, :]

        def probs_t(i):
            return probs_g[:, 2 + i % 2, :].rearrange("p (b c) -> p b c", c=P)

        def ub_bank(j, half):
            return 4 + (NH * j + half) % 4

        def ht_bank(j):
            return 2 * (j % 2)

        with nc.Fori(0, B) as image:
            with nc.Block() as block:

                @block.sync
                def _(sp):
                    sp.dma_start(x_in[:], I["x"][image]).then_inc(x_loaded, 16)
                    sp.wait_ge(out_kept, 1)
                    sp.dma_start(out[image], out_s).then_inc(stored, 16)
                    sp.wait_ge(stored, 16)

                @block.tensor
                def _(pe):
                    def mm(o, a, b, first=True, last=True):
                        return nc.tensor.matmul(o, a, b, start=first, stop=last)

                    def turn_blocks(src, bank):
                        for i in range(NB):
                            t = nc.tensor.transpose(banks(bank, 2)[:, i * P:(i + 1) * P], src[:, i, :], ident[:])
                        return t

                    pe.wait_ge(x_loaded, 16)
                    for i in range(NB):
                        t = nc.tensor.transpose(banks(0, 2)[:, i * C:(i + 1) * C], x_in[:, i * P:(i + 1) * P], ident[:])
                    t.then_inc(xt_made, 1)
                    for w, bank, made in ((wq, 2, q_made), (wk, 4, k_made)):
                        for c in range(NCH):
                            t = mm(ps[:, bank + c, :], w[:], x_in[:, c * BANK:(c + 1) * BANK])
                        t.then_inc(made, 1)
                    for i in range(NB):
                        t = mm(banks(6, 2)[:, i * C:(i + 1) * C], x_in[:, i * P:(i + 1) * P], wv[:])
                    t.then_inc(v_made, 1)

                    def score(i):
                        for c in range(NCH):
                            t = mm(ps[:, 2 * (i % 2) + c, :], q[:, i * P:(i + 1) * P], k[:, c * BANK:(c + 1) * BANK])
                        t.then_inc(scores_made, 1)

                    pe.wait_ge(xt_kept, 1)
                    pe.wait_ge(qkv_kept, 2)
                    score(0)
                    score(1)
                    pe.wait_ge(qkv_kept, 3)
                    for i in range(NB):
                        pe.wait_ge(probs_made, i + 1)
                        if i >= 1:
                            pe.wait_ge(probs_kept, i)
                        for j in range(NB):
                            t = nc.tensor.transpose(banks(4, 2)[:, j * P:(j + 1) * P],
                                                    probs(i)[:, j * P:(j + 1) * P], ident[:])
                        t.then_inc(probs_turned, 1)
                        if i + 2 < NB:
                            score(i + 2)
                        pe.wait_ge(probs_kept, i + 1)
                        if i >= 2:
                            pe.wait_ge(t1_made, i - 1)
                        for j in range(NB):
                            t = mm(ps[:, 6 + i % 2, 0:C], probs_t(i)[:, j, :], v_tok[:, j, :], j == 0, j == NB - 1)
                        t.then_inc(attn_made, 1)

                    pe.wait_ge(ln_made[0], NB)
                    turn_blocks(normed, 0).then_inc(ln_turned[0], 1)

                    for r in range(DIRS):
                        src = (x_fwd, x_bwd)[r]
                        pe.wait_ge(ln_kept[0], r + 1)
                        if r == 0:
                            pe.wait_ge(ln_kept[0], 2)
                        else:
                            pe.wait_ge(y_added, r * STEPS * QB)
                        for half in range(NH):
                            for c in range(NCH):
                                for tap in range(KCONV):
                                    t = mm(ps[:, NCH * half + c, :], cw_rows[:, r, tap, half * P:(half + 1) * P],
                                           src[:, tap + c * BANK:tap + (c + 1) * BANK], tap == 0, tap == KCONV - 1)
                            t.then_inc(xc_made, 1)
                        if r > 0:
                            pe.wait_ge(y_skip, r * NH)
                        for half in range(NH):
                            for c in range(NCH):
                                t = mm(ps[:, 4 + NCH * half + c, :], w_in[:, r, DI + half * P:DI + (half + 1) * P],
                                       src[:, PAD + c * BANK:PAD + (c + 1) * BANK])
                            t.then_inc(z_made, 1)
                        pe.wait_ge(xc_kept, NH * (r + 1))
                        for c in range(NCH):
                            for half in range(NH):
                                t = mm(ps[0:DR, c, :], w_x[:, r, half, 0:DR],
                                       xc[:, half, c * BANK:(c + 1) * BANK], half == 0, half == NH - 1)
                        t.then_inc(dt16_made, 1)
                        for i in range(NB):
                            for half in range(NH):
                                t = mm(ps[:, 2, i * 2 * DS:(i + 1) * 2 * DS], xc[:, half, i * P:(i + 1) * P],
                                       w_x[:, r, half, DR:DR + 2 * DS], half == 0, half == NH - 1)
                        t.then_inc(bc_made, 1)
                        pe.wait_ge(dt16_kept, r + 1)
                        pe.wait_ge(z_kept, NH * (r + 1))
                        for half in range(NH):
                            for c in range(NCH):
                                t = mm(ps[:, 4 + NCH * half + c, :], w_dt[:, r, half * P:(half + 1) * P],
                                       dt16[:, c * BANK:(c + 1) * BANK])
                            t.then_inc(dt_made, 1)
                        pe.wait_ge(bc_kept, r + 1)
                        pe.wait_ge(u_made, NH * (r + 1))
                        for i in range(NB):
                            for half in range(NH):
                                t = nc.tensor.transpose(
                                    banks(0, 4)[:, (NH * i + half) * P:(NH * i + half + 1) * P],
                                    u[:, half, i * P:(i + 1) * P], ident[:])
                            if i % QB == QB - 1:
                                t.then_inc(u_turned, 1)

                        def turn_ub(j):
                            n = r * STEPS + j
                            pe.wait_ge(ub_made, QB * (n + 1))
                            for half in range(NH):
                                if j >= 2:
                                    pe.wait_ge(h_made, NH * (n - 2) + half + 1)
                                for b in range(QB):
                                    t = nc.tensor.transpose(ps[:, ub_bank(j, half), b * P:(b + 1) * P],
                                                            ub[:, j % RING, b, half * P:(half + 1) * P], ident[:])
                                t.then_inc(ub_turned, 1)

                        def turn_h(j):
                            n = r * STEPS + j
                            pe.wait_ge(h_made, NH * (n + 1))
                            if j == 0:
                                pe.wait_ge(u_kept, 2 * (r + 1))
                            if j >= 2:
                                pe.wait_ge(y_added, QB * (n - 1))
                            for b in range(QB):
                                for half in range(NH):
                                    t = nc.tensor.transpose(
                                        banks(ht_bank(j), 2)[:, (NH * b + half) * P:(NH * b + half + 1) * P],
                                        h[:, j % RING, half, b * P:(b + 1) * P], ident[:])
                                if b % 2 == 1:
                                    t.then_inc(h_turned, 1)

                        pe.wait_ge(dt_kept, NH * (r + 1))
                        turn_ub(0)
                        turn_ub(1)
                        for j in range(STEPS):
                            turn_h(j)
                            if j + 2 < STEPS:
                                turn_ub(j + 2)
                        pe.wait_ge(y_added, (r + 1) * STEPS * QB)
                        for half in range(NH):
                            for i in range(NB):
                                t = nc.tensor.transpose(banks(4 + 2 * half, 2)[:, i * P:(i + 1) * P],
                                                        y_tok[:, i, half * P:(half + 1) * P], ident[:])
                            t.then_inc(y_turned, 1)

                    pe.wait_ge(y_gated, DIRS * NH)
                    for i in range(NB):
                        for r in range(DIRS):
                            for half in range(NH):
                                t = mm(banks(0, 2)[:, i * C:(i + 1) * C], y[:, r, half, i * P:(i + 1) * P],
                                       w_out[:, r, half, :], r + half == 0, r + half == DIRS + NH - 2)
                    t.then_inc(m_made, 1)
                    pe.wait_ge(ln_made[1], NB)
                    turn_blocks(normed, 2).then_inc(ln_turned[1], 1)
                    pe.wait_ge(ln_kept[1], 1)
                    for o in range(HM):
                        for c in range(NCH):
                            t = mm(ps[:, 4 + NCH * o + c, :], w1[:, o * P:(o + 1) * P], h1[:, c * BANK:(c + 1) * BANK])
                        t.then_inc(hid1_made, 1)
                    pe.wait_ge(hid1_leaky, HM)
                    for i in range(NB):
                        for o in range(HM):
                            mm(banks(0, 2)[:, i * C:(i + 1) * C], act1[:, o, i * P:(i + 1) * P], w2[:, o, :],
                               o == 0, False)
                        t = mm(banks(0, 2)[:, i * C:(i + 1) * C], ones_row[:], b2[:], False, True)
                    t.then_inc(mlp_made, 1)

                    pe.wait_ge(ln_made[2], NB)
                    turn_blocks(n2, 2).then_inc(ln_turned[2], 1)
                    pe.wait_ge(ln_kept[2], 1)
                    pe.wait_ge(t2_made, 1)
                    for c in range(NCH):
                        t = mm(ps[:, c, :], wr_cols[:], n2c[:, c * BANK:(c + 1) * BANK])
                    t.then_inc(w_made, 1)

                    def hidden(o):
                        for c in range(NCH):
                            t = mm(ps[:, 4 + 2 * (o % 2) + c, :], f_w1[:, o * P:(o + 1) * P],
                                   n2c[:, c * BANK:(c + 1) * BANK])
                        t.then_inc(hid2_made, 1)

                    hidden(0)
                    hidden(1)
                    pe.wait_ge(w_kept_row, 1)
                    for i in range(NB):
                        t = nc.tensor.transpose(ps[:, 2, i:i + 1], w_row[0:1, i * P:(i + 1) * P], ident[0:1, 0:1])
                    t.then_inc(w_turned, 1)
                    for o in range(2, HF):
                        pe.wait_ge(hid2_kept, o - 1)
                        hidden(o)
                    pe.wait_ge(hid2_kept, HF)
                    for i in range(NB):
                        for o in range(HF):
                            mm(banks(0, 2)[:, i * C:(i + 1) * C], probs_g[:, o, i * P:(i + 1) * P], f_w2[:, o, :],
                               o == 0, False)
                        t = mm(banks(0, 2)[:, i * C:(i + 1) * C], ones_row[:], f_b2[:], False, True)
                    t.then_inc(ffn_made, 1)
                    pe.wait_ge(t3_made, NB)
                    pe.wait_ge(w_col_kept, 1)
                    turn_blocks(normed, 2).then_inc(out_turned, 1)

                @block.scalar
                def _(act):
                    act.wait_ge(q_made, 1)
                    act.activation(q[:], banks(2, 2), ACT.Identity, bias=bq[:], scale=SCALE).then_inc(qkv_kept, 1)
                    act.wait_ge(k_made, 1)
                    act.activation(k[:], banks(4, 2), ACT.Identity, bias=bk[:]).then_inc(qkv_kept, 1)
                    act.wait_ge(v_made, 1)
                    act.activation(v_tok[:], blocks(6), ACT.Copy).then_inc(qkv_kept, 1)

                    def softmax(i):
                        act.wait_ge(max_made, i + 1)
                        if i >= 2:
                            act.wait_ge(probs_turned, i - 1)
                        act.activation(probs(i), banks(2 * (i % 2), 2), ACT.Exp, bias=nmax[:, i:i + 1],
                                       accum_out=rowsum[:, i:i + 1]).then_inc(probs_made, 1)

                    softmax(0)
                    for i in range(NB):
                        if i + 1 < NB:
                            softmax(i + 1)
                        act.wait_ge(probs_turned, i + 1)
                        if i >= 2:
                            act.wait_ge(attn_made, i - 1)
                        act.activation(probs_t(i), blocks(4), ACT.Copy).then_inc(probs_kept, 1)

                    act.wait_ge(ln_turned[0], 1)
                    act.activation(x_fwd[:, PAD:], banks(0, 2), ACT.Copy).then_inc(ln_kept[0], 1)
                    act.activation(x_bwd[:, PAD:][:, ::-1], banks(0, 2), ACT.Copy).then_inc(ln_kept[0], 1)

                    for r in range(DIRS):
                        if r > 0:
                            act.wait_ge(y_skip, r * NH)
                        for half in range(NH):
                            act.wait_ge(xc_made, r * NH + half + 1)
                            act.activation(xc[:, half, :], banks(2 * half, 2), ACT.Silu,
                                           bias=conv_b[:, r, half:half + 1]).then_inc(xc_kept, 1)
                        if r > 0:
                            act.wait_ge(y_gated, r * NH)
                        for half in range(NH):
                            act.wait_ge(z_made, r * NH + half + 1)
                            act.activation(sz[:, half, :], banks(4 + 2 * half, 2), ACT.Silu).then_inc(z_kept, 1)
                        if r > 0:
                            act.wait_ge(y_turned, r * NH)
                        for half in range(NH):
                            act.wait_ge(dt_made, r * NH + half + 1)
                            act.activation(u[:, half, :], banks(4 + 2 * half, 2), ACT.Exp,
                                           bias=b_dt[:, r, half:half + 1]).then_inc(dt_exp, 1)
                        for half in range(NH):
                            act.wait_ge(dt_cut, r * NH + half + 1)
                            act.activation(u[:, half, :], u[:, half, :], ACT.Ln, bias=1.0).then_inc(dt_log, 1)
                        for n in range(2):
                            act.wait_ge(u_turned, 2 * r + n + 1)
                            if r > 0 and n == 0:
                                act.wait_ge(ub_made, r * STEPS * QB)
                            act.activation(u_tok[:, QB * n:QB * (n + 1), :].rearrange("p b d -> p (b d)"),
                                           banks(2 * n, 2), ACT.Copy).then_inc(u_kept, 1)
                        act.wait_ge(dt_kept, NH * (r + 1))
                        for s in range(DS):
                            for half in range(NH):
                                n = r * STEPS + NCH * s
                                if s >= 2:
                                    act.wait_ge(h_made, NH * (n - NCH - 1) + half + 1)
                                elif r > 0:
                                    act.wait_ge(h_made, NH * r * STEPS)
                                act.activation(da[:, s % 2, half, :], dt[:, half, :], ACT.Exp,
                                               scale=a_neg[:, r, half, s:s + 1]).then_inc(da_made, 1)

                    act.wait_ge(m_made, 1)
                    act.activation(m, blocks(0), ACT.Copy).then_inc(m_kept, 1)
                    act.wait_ge(ln_turned[1], 1)
                    act.activation(h1, banks(2, 2), ACT.Identity, bias=ln_b[:], scale=ln_g[:]).then_inc(ln_kept[1], 1)
                    for o in range(HM):
                        act.wait_ge(hid1_made, o + 1)
                        act.activation(act1[:, o, :], banks(4 + 2 * o, 2), ACT.Identity,
                                       bias=b1[:, o:o + 1]).then_inc(hid1_kept, 1)
                    act.wait_ge(ln_turned[2], 1)
                    act.activation(n2c, banks(2, 2), ACT.Copy).then_inc(ln_kept[2], 1)
                    act.wait_ge(w_made, 1)
                    act.activation(w_row, banks(0, 2), ACT.Identity, bias=br[:]).then_inc(w_kept_row, 1)
                    for o in range(HF):
                        act.wait_ge(hid2_made, o + 1)
                        act.activation(probs_g[:, o, :], banks(4 + 2 * (o % 2), 2), ACT.Gelu_apprx_tanh,
                                       bias=f_b1[:, o:o + 1]).then_inc(hid2_kept, 1)
                    act.wait_ge(out_turned, 1)
                    act.activation(out_s, banks(2, 2), ACT.Copy).then_inc(out_kept, 1)

                @block.gpsimd
                def _(pool):
                    def inverse_deviation(n):
                        pool.wait_ge(ln_var[n], NB)
                        pool.tensor_scalar(var_eps[:], mean_var[:, :, 1], EPS, None, ALU.add).then_inc(ln_eps[n], 1)
                        pool.wait_ge(ln_eps[n], 1)
                        pool.tensor_tensor(rstd[:], var_eps[:], minus_half[:], ALU.pow).then_inc(ln_rstd[n], 1)

                    inverse_deviation(0)
                    for r in range(DIRS):
                        for half in range(NH):
                            pool.wait_ge(dt_kept, r * NH + half + 1)
                            pool.tensor_tensor(u[:, half, :], dt[:, half, :], xc[:, half, :], ALU.mult).then_inc(u_made, 1)
                        for j in range(STEPS):
                            n = r * STEPS + j
                            s, c = divmod(j, NCH)
                            if j == 0:
                                pool.wait_ge(bc_kept, r + 1)
                            if j < NCH:
                                pool.wait_ge(u_kept, 2 * r + c + 1)
                            if n >= RING:
                                pool.wait_ge(ub_turned, NH * (n - RING + 1))
                            for b in range(QB):
                                pool.tensor_scalar(ub[:, j % RING, b, :], u_tok[:, QB * c + b, :],
                                                   bc[:, QB * c + b, s:s + 1], 1.0, ALU.mult, ALU.mult
                                                   ).then_inc(ub_made, 1)
                        for half in range(NH):
                            pool.wait_ge(y_skip, r * NH + half + 1)
                            pool.tensor_tensor(y[:, r, half, :], y[:, r, half, :], sz[:, half, :], ALU.mult
                                               ).then_inc(y_gated, 1)
                    inverse_deviation(1)
                    pool.wait_ge(m_kept, 1)
                    pool.tensor_tensor(mt, m, t1[:], ALU.add).then_inc(mt_made, 1)
                    inverse_deviation(2)
                    pool.wait_ge(ln_made[2], NB)
                    pool.tensor_tensor(t1[:], t2, n2, ALU.add).then_inc(base_made, 1)

                @block.vector
                def _(dve):
                    def layer_norm(n, src, dst):
                        for i in range(NB):
                            dve.bn_stats(stats[:, i, :], src[:, i, :]).then_inc(ln_stats[n], 1)
                        for i in range(NB):
                            dve.wait_ge(ln_stats[n], i + 1)
                            dve.bn_aggr(mean_var[:, i, :], stats[:, i, :]).then_inc(ln_var[n], 1)
                        dve.wait_ge(ln_rstd[n], 1)
                        for i in range(NB):
                            dve.tensor_scalar(dst[:, i, :], src[:, i, :], mean_var[:, i, 0:1], rstd[:, i:i + 1],
                                              ALU.subtract, ALU.mult).then_inc(ln_made[n], 1)

                    dve.wait_ge(xt_made, 1)
                    dve.tensor_tensor(x_tok[:], blocks(0), bv_rows[:].unsqueeze(1).to_broadcast([P, NB, C]), ALU.add
                                      ).then_inc(xt_kept, 1)

                    def row_max(i):
                        dve.wait_ge(scores_made, i + 1)
                        dve.tensor_reduce(nmax[:, i:i + 1], banks(2 * (i % 2), 2), AX.X, ALU.max, negate=True
                                          ).then_inc(max_made, 1)

                    row_max(0)
                    row_max(1)
                    for i in range(NB):
                        if i + 2 < NB:
                            row_max(i + 2)
                        dve.wait_ge(probs_made, i + 1)
                        dve.reciprocal(rinv[:, i:i + 1], rowsum[:, i:i + 1]).then_inc(rinv_made, 1)
                        dve.wait_ge(rinv_made, i + 1)
                        dve.wait_ge(attn_made, i + 1)
                        dve.scalar_tensor_tensor(t1[:, i, :], ps[:, 6 + i % 2, 0:C], rinv[:, i:i + 1], x_tok[:, i, :],
                                                 ALU.mult, ALU.add).then_inc(t1_made, 1)
                    dve.wait_ge(t1_made, NB)
                    layer_norm(0, t1, normed)

                    for r in range(DIRS):
                        dve.wait_ge(dt16_made, r + 1)
                        dve.tensor_copy(dt16[:], banks(0, 2)[0:DR, :]).then_inc(dt16_kept, 1)
                        dve.wait_ge(bc_made, r + 1)
                        dve.tensor_copy(bc[:].rearrange("p b s -> p (b s)"), ps[:, 2, 0:NB * 2 * DS]).then_inc(bc_kept, 1)
                        for half in range(NH):
                            dve.wait_ge(dt_exp, r * NH + half + 1)
                            dve.tensor_scalar(u[:, half, :], u[:, half, :], EXP_MAX, None, ALU.min).then_inc(dt_cut, 1)
                        for half in range(NH):
                            dve.wait_ge(dt_log, r * NH + half + 1)
                            dve.scalar_tensor_tensor(dt[:, half, :], banks(4 + 2 * half, 2), b_dt[:, r, half:half + 1],
                                                     u[:, half, :], ALU.add, ALU.max).then_inc(dt_kept, 1)

                        def scan(j):
                            n = r * STEPS + j
                            s, c = divmod(j, NCH)
                            for half in range(NH):
                                if c == 0:
                                    dve.wait_ge(da_made, NH * (r * DS + s) + half + 1)
                                    before = 0.0
                                else:
                                    dve.wait_ge(h_made, NH * (n - 1) + half + 1)
                                    before = h[:, (j - 1) % RING, half, BANK - 1:BANK]
                                dve.wait_ge(ub_turned, NH * n + half + 1)
                                if n >= RING and half == 0:
                                    dve.wait_ge(h_turned, 2 * (n - RING + 1))
                                dve.tensor_tensor_scan(h[:, j % RING, half, :],
                                                       da[:, s % 2, half, c * BANK:(c + 1) * BANK],
                                                       ps[:, ub_bank(j, half), :], before, ALU.mult, ALU.add
                                                       ).then_inc(h_made, 1)

                        def add_y(j):
                            n = r * STEPS + j
                            s, c = divmod(j, NCH)
                            for b in range(QB):
                                i = QB * c + b
                                if b % 2 == 0:
                                    dve.wait_ge(h_turned, 2 * n + b // 2 + 1)
                                src = banks(ht_bank(j), 2)[:, b * DI:(b + 1) * DI]
                                weight = bc[:, i, DS + s:DS + s + 1]
                                if s == 0:
                                    if j == 0 and b == 0:
                                        dve.wait_ge(u_turned, 2 * (r + 1))
                                    dve.tensor_scalar(y_tok[:, i, :], src, weight, None, ALU.mult).then_inc(y_added, 1)
                                else:
                                    dve.wait_ge(y_added, QB * (n - NCH) + b + 1)
                                    dve.scalar_tensor_tensor(y_tok[:, i, :], src, weight, y_tok[:, i, :],
                                                             ALU.mult, ALU.add).then_inc(y_added, 1)

                        scan(0)
                        for j in range(1, STEPS):
                            scan(j)
                            add_y(j - 1)
                        add_y(STEPS - 1)
                        for half in range(NH):
                            dve.wait_ge(y_turned, r * NH + half + 1)
                            dve.scalar_tensor_tensor(y[:, r, half, :], xc[:, half, :], d_skip[:, r, half:half + 1],
                                                     banks(4 + 2 * half, 2), ALU.mult, ALU.add).then_inc(y_skip, 1)

                    dve.wait_ge(m_kept, 1)
                    layer_norm(1, m, normed)
                    for o in range(HM):
                        dve.wait_ge(hid1_kept, o + 1)
                        dve.scalar_tensor_tensor(act1[:, o, :], act1[:, o, :], SLOPE, act1[:, o, :],
                                                 ALU.mult, ALU.max).then_inc(hid1_leaky, 1)
                    dve.wait_ge(mt_made, 1)
                    dve.wait_ge(mlp_made, 1)
                    dve.tensor_tensor(t2, blocks(0), mt, ALU.add).then_inc(t2_made, 1)
                    dve.wait_ge(t2_made, 1)
                    layer_norm(2, t2, n2)

                    dve.wait_ge(w_turned, 1)
                    dve.tensor_copy(w_col[:], ps[:, 2, 0:NB]).then_inc(w_col_kept, 1)
                    dve.wait_ge(w_col_kept, 1)
                    dve.wait_ge(w_kept_row, 1)
                    done = 0
                    for i in range(NB):
                        mine = w_col[:, i:i + 1]
                        parts = [(2, slice(i * P, (i + 1) * P)), (1, slice(i * P, T))]
                        if i:
                            parts.append((0, slice(0, i * P)))
                        for kind, cols in parts:
                            if done:
                                dve.wait_ge(compared, done)
                            if kind == 2:
                                t = dve.scalar_tensor_tensor(junk[:, cols], w_row[:, cols], mine, below[:],
                                                             ALU.is_equal, ALU.mult, accum_out=counts[:, i, 2:3])
                            else:
                                t = dve.tensor_scalar(junk[:, cols], w_row[:, cols], mine, None,
                                                      (ALU.is_ge, ALU.is_gt)[kind], ALU.add,
                                                      accum_out=counts[:, i, kind:kind + 1])
                            t.then_inc(compared, 1)
                            done += 1
                    dve.wait_ge(compared, done)
                    dve.tensor_reduce(rank[:], counts[:], AX.X, ALU.add).then_inc(ranked, 1)
                    dve.wait_ge(ranked, 1)
                    dve.scalar_tensor_tensor(w_kept[:], rank[:], float(KEPT), w_col[:], ALU.is_lt, ALU.mult
                                             ).then_inc(wk_made, 1)
                    dve.wait_ge(wk_made, 1)
                    dve.wait_ge(base_made, 1)
                    dve.wait_ge(ffn_made, 1)
                    for i in range(NB):
                        dve.scalar_tensor_tensor(normed[:, i, :], blocks(0)[:, i, :], w_kept[:, i:i + 1], t1[:, i, :],
                                                 ALU.mult, ALU.add).then_inc(t3_made, 1)

            nums = [s.num for s in first_sem]
            nc.all_engine_barrier(sems_to_clear=range(min(nums), max(nums) + 1))

def kernel(**inputs):
    import concourse.bacc as _bacc
    from concourse import mybir as _mybir
    from concourse.bass_utils import run_bass_kernel_spmd as _run

    a = {k: np.asarray(v) for k, v in inputs.items()}
    P = 128

    def columns(v):
        return np.moveaxis(v.reshape(*v.shape[:-1], v.shape[-1] // P, P), -1, 0)

    x = a["x"]
    B, C, H, W = x.shape
    m = {k.removeprefix("L1_attn_"): v for k, v in a.items() if k.startswith("L1_attn_")}
    f = {k.removeprefix("L1_ffn_"): v for k, v in a.items() if k.startswith("L1_ffn_")}
    DIRS, DI, KCONV = m["conv_w"].shape
    laid = {
        "x": x.reshape(B, C, H * W),
        "wq": a["L0_conv_Wq"].T, "wk": a["L0_conv_Wk"].T, "wv": a["L0_conv_Wv"].T,
        "bq": a["L0_conv_bq"].reshape(C, 1), "bk": a["L0_conv_bk"].reshape(C, 1),
        "bv": a["L0_conv_bv"].reshape(1, C),
        "in_proj": m["in_proj_w"].transpose(0, 2, 1),
        "conv_rows": m["conv_w"].transpose(0, 2, 1).reshape(1, -1),
        "conv_b": columns(m["conv_b"]),
        "x_proj": columns(m["x_proj_w"]).transpose(0, 1, 3, 2),
        "dt_w": m["dt_proj_w"].transpose(2, 0, 1),
        "dt_b": columns(m["dt_proj_b"]),
        "A_logs": columns(m["A_log"].transpose(0, 2, 1)).transpose(0, 1, 3, 2),
        "Dp": columns(m["Dp"]),
        "out_w": columns(m["out_proj_w"]).transpose(0, 1, 3, 2),
        "ln_g": m["ln_g"].reshape(C, 1), "ln_b": m["ln_b"].reshape(C, 1),
        "w1": m["w1"].T, "b1": columns(m["b1"]),
        "w2": columns(m["w2"]).transpose(0, 2, 1), "b2": m["b2"].reshape(1, C),
        "wr": f["wr"].reshape(C, 1), "br": f["br"].reshape(1, 1),
        "f_w1": f["w1"], "f_b1": columns(f["b1"]),
        "f_w2": columns(f["w2"].T).transpose(0, 2, 1), "f_b2": f["b2"].reshape(1, C),
    }
    shapes = {"conv_w": m["conv_w"], "A_log": m["A_log"], "dt_proj_w": m["dt_proj_w"]}

    nc = _bacc.Bacc("TRN2", target_bir_lowering=False, num_devices=1)
    arrays, args = {}, {}
    for name, v in laid.items():
        v = np.ascontiguousarray(v)
        arrays[f"in_{name}"] = v
        args[name] = nc.dram_tensor(f"in_{name}", v.shape, _mybir.dt.from_np(v.dtype), kind="ExternalInput").ap()
    args.update(shapes)
    out = nc.dram_tensor("out", (B, C, H * W), _mybir.dt.float32, kind="ExternalOutput").ap()
    conv_attn_mamba_mod_kernel(nc, args, out)
    r = _run(nc, [arrays], core_ids=[0])
    return r.results[0]["out"].reshape(B, C, H, W)
```

```python
import concourse.bass as bass
from concourse import mybir
from contextlib import ExitStack
import numpy as np

def conv_attn_mamba_mod_kernel(nc, I, out):
    fp32 = mybir.dt.float32
    bf16 = mybir.dt.bfloat16
    ALU = mybir.AluOpType
    ACT = mybir.ActivationFunctionType
    AX = mybir.AxisListType

    B, C, T = I["x"].shape
    P = 128
    NB = T // P
    BANK = 512
    NCH = T // BANK
    QB = BANK // P
    DIRS, DI, KCONV = I["conv_w"].shape
    NH = DI // P
    DS = I["A_log"].shape[2]
    DR = I["dt_proj_w"].shape[2]
    HM = I["w1"].shape[1] // P
    HF = I["f_w1"].shape[1] // P
    PAD = KCONV - 1
    KEPT = T // 2 - 1
    SCALE = float(np.float32(1.0) / np.sqrt(np.float32(C)))
    EPS = 1e-5
    SLOPE = 0.01
    EXP_MAX = 1e15
    STEPS = DS * NCH
    ALL = DIRS * STEPS
    QUAD = 32
    BROWS = 2 * QUAD + DS
    DTROW = 3 * QUAD
    XROWS = DTROW + DR

    LEAD_BC, LEAD_KEPT, LEAD_DBX = 3, 2, 1

    HB, BB, Z, X, Y = 0, 2, 3, 4, 6

    AT_YT = {1: (0, 1), 0: (65, 65)}
    AT_SKIP = {1: (2, 3), 0: (67, 68)}
    STEP_GATE = {1: 2, 0: 35}
    AT_M1 = (9, 13)
    AT_MSUM = (10, 14)
    LN_STATS, LN_AGGR, LN_APPLY = {0: 96, 1: 15, 2: 35}, {0: 97, 1: 16, 2: 37}, {0: 100, 1: 21, 2: 42}
    LN_TURN, LN_KEEP, STEP_LN = {0: 101, 1: 25, 2: 44}, {0: 102, 1: 26, 2: 45}, {0: 49, 1: 9, 2: 19}
    AT_W1, AT_HID1, AT_LEAKY = (27, 28), (28, 29), (29, 30)
    AT_W2, AT_T2 = (32, 33), 34
    STEP_MT, STEP_B2, STEP_BASE = (8, 10), (11, 12), (22, 23)
    AT_W, AT_WKEEP, AT_WTURN, AT_WCOL = 46, 47, 48, 49
    AT_HID, AT_GELU = (47, 49, 51, 52), (50, 53)
    AT_RANK, AT_WK = 50, 58
    AT_FFN, AT_T3, AT_OUT, AT_OUTKEEP = 54, (59, 60), 61, 62
    AT_T1OLD = 30
    AT_XT, AT_XTOK, AT_Q, AT_K, AT_V, AT_QKEEP, AT_KKEEP, AT_VKEEP = 4, 5, 5, 6, 8, 6, 7, 9
    AT_S = [61] + [65 + 3 * i for i in range(1, NB)]
    AT_MAX = [n + 1 for n in AT_S]
    AT_EXP = [n + 2 for n in AT_S]
    AT_PT = [69 + 3 * i for i in range(NB)]
    AT_PTKEEP = [n + 2 for n in AT_PT]
    AT_PV = [n + 4 for n in AT_PT]
    AT_T1 = [n + 5 for n in AT_PT]
    AT_Z, AT_ZKEEP = {0: (10, 11), 1: (89, 93)}, {0: 14, 1: 94}
    AT_M0, AT_M0KEEP = (95, 96), 97
    AT_CONV = {1: (15, 16, 17, 18, 19, 20, 22, 23), 0: tuple(range(103, 111))}
    AT_XC = {1: 24, 0: 111}
    AT_ROWS, AT_ROWKEEP = {1: (26, 29), 0: (112, 114)}, {1: (27, 30), 0: (113, 115)}
    AT_C, AT_CKEEP = {1: 31, 0: 116}, {1: 32, 0: 117}
    AT_BHI, AT_BR1, AT_BMID, AT_BR2, AT_BLO = {1: 31, 0: 116}, {1: 32, 0: 117}, {1: 33, 0: 118}, {1: 34, 0: 119}, {1: 35, 0: 120}
    AT_DT, AT_DTEXP = {1: (34, 36), 0: (116, 117)}, {1: (35, 37), 0: (117, 118)}
    AT_CUT, AT_LOG, AT_DTMAX = {1: (36, 38), 0: (118, 119)}, {1: (38, 39), 0: (119, 120)}, {1: (40, 41), 0: (120, 121)}
    STEP_U = {1: (24, 25, 26, 27), 0: (60, 61, 63, 63)}

    ctx = ExitStack()
    with ctx:
        def sb(name, shape, dtype=fp32):
            return ctx.enter_context(nc.sbuf_tensor(name, shape, dtype))

        turn_sems = []

        def sem(name):
            s = ctx.enter_context(nc.semaphore(name))
            turn_sems.append(s)
            return s

        ident = sb("ident", [P, P])
        below = sb("below", [P, P])
        pick = sb("pick", [BROWS, DS], bf16)
        ones_row = sb("ones_row", [1, P])
        wq = sb("wq", [C, C])
        wk = sb("wk", [C, C])
        wv = sb("wv", [C, C])
        bq = sb("bq", [C, 1])
        bk = sb("bk", [C, 1])
        bv_rows = sb("bv_rows", [P, C])
        w_z = sb("w_z", [C, DIRS, DI])
        w_conv = sb("w_conv", [C, DIRS, KCONV, DI])
        conv_b = sb("conv_b", [P, DIRS, NH])
        w_rows = sb("w_rows", [P, DIRS, NH, XROWS])
        w_c = sb("w_c", [P, DIRS, NH, DS])
        w_dt = sb("w_dt", [XROWS, DIRS, DI])
        b_dt = sb("b_dt", [P, DIRS, NH])
        a_neg = sb("a_neg", [P, DIRS, NH, DS])
        d_skip = sb("d_skip", [P, DIRS, NH])
        w_out = sb("w_out", [P, DIRS, NH, C])
        ln_g = sb("ln_g", [C, 1])
        ln_b = sb("ln_b", [C, 1])
        w1 = sb("w1", [C, HM * P])
        b1 = sb("b1", [P, HM])
        w2 = sb("w2", [P, HM, C])
        b2_rows = sb("b2_rows", [P, C])
        wr = sb("wr", [C, 1])
        wr_cols = sb("wr_cols", [C, P])
        br = sb("br", [P, 1])
        f_w1 = sb("f_w1", [C, HF * P])
        f_b1 = sb("f_b1", [P, HF])
        f_w2 = sb("f_w2", [P, HF, C])
        f_b2 = sb("f_b2", [1, C])
        minus_half = sb("minus_half", [P, NB])

        q = sb("q", [C, T])
        k = sb("k", [C, T])
        v_tok = sb("v_tok", [P, NB, C])
        x_tok = sb("x_tok", [P, NB, C])
        nmax = sb("nmax", [P, NB])
        rowsum = sb("rowsum", [P, NB])
        rinv = sb("rinv", [P, NB])
        t1 = sb("t1", [P, NB, C])
        t1_old = sb("t1_old", [P, NB, C])
        stats = sb("stats", [P, NB, 6])
        mean_var = sb("mean_var", [P, NB, 2])
        var_eps = sb("var_eps", [P, NB])
        rstd = sb("rstd", [P, NB])
        x_pad = sb("x_pad", [C, PAD + T + PAD])
        xc = sb("xc", [P, DIRS, NH, T])
        dt = sb("dt", [P, DIRS, NH, T])
        u = sb("u", [P, DIRS, NH, T])
        sz = sb("sz", [P, NH, T])
        rows = sb("rows", [XROWS, T])
        b_parts = sb("b_parts", [BROWS, DIRS, T], bf16)
        c_tok = sb("c_tok", [P, DIRS, NB, DS])
        b_all = sb("b_all", [P, 2, BANK])
        dbx = sb("dbx", [P, 2, NH, BANK])
        da = sb("da", [P, 2, NH, T])
        h = sb("h", [P, 2, NH, BANK])
        y_tok = sb("y_tok", [P, NB, DI])
        m0 = sb("m0", [P, NB, C])
        res = sb("res", [P, NB, C])
        tile_a = sb("tile_a", [P, T])
        tile_b = sb("tile_b", [P, T])
        tile_c = sb("tile_c", [P, T])
        hid = sb("hid", [P, HF, T])
        w_col = sb("w_col", [P, NB])
        counts = sb("counts", [P, NB, 3])
        rank = sb("rank", [P, NB])
        w_kept = sb("w_kept", [P, NB])

        def by_block(tile):
            return tile.rearrange("p (b c) -> p b c", c=C)

        m, n2, junk, probs_t = by_block(tile_a[:, :]), by_block(tile_a[:, :]), tile_a[:, :], by_block(tile_a[:, :])
        m_normed, n2c, out_s = by_block(tile_b[:, :]), tile_b[:, :], tile_b[:, :]
        x_in, w_row, probs = tile_c[:, :], tile_c[:, :], tile_c[:, :]
        h1 = hid[:, HM, :]
        in_cols = hid[:, 0:DIRS * DI // T + 1, :].rearrange("p a t -> p (a t)")[:, 0:DIRS * DI].rearrange(
            "p (r e) -> p r e", r=DIRS)
        ln_tile = {0: (t1, x_tok), 1: (m, m_normed), 2: (res, n2)}

        ps = ctx.enter_context(nc.psum_tensor("ps", [P, 8, BANK], fp32))

        def banks(n):
            return ps[:, n:n + 2, :].rearrange("p b c -> p (b c)")

        def blocks(n):
            return by_block(banks(n))

        def cols(c):
            return slice(c * BANK, (c + 1) * BANK)

        loaded = ctx.enter_context(nc.semaphore("loaded"))
        zeroed = ctx.enter_context(nc.semaphore("zeroed"))
        picked = ctx.enter_context(nc.semaphore("picked"))
        setup_exp = ctx.enter_context(nc.semaphore("setup_exp"))

        with nc.Block() as block:
            loads = [
                (wq[:], I["wq"]), (wk[:], I["wk"]), (wv[:], I["wv"]),
                (bq[:], I["bq"]), (bk[:], I["bk"]),
                (bv_rows[:], I["bv"].to_broadcast([P, C])),
                (in_cols, I["in_proj"][:, :, 0:DI].rearrange("r c e -> c r e")),
                (w_z[:], I["in_proj"][:, :, DI:2 * DI].rearrange("r c e -> c r e")),
                (w_conv[:].rearrange("p r k e -> p (r k e)"), I["conv_rows"].to_broadcast([P, DIRS * KCONV * DI])),
                (conv_b[:], I["conv_b"]),
                (w_c[:], I["x_proj"][:, :, :, DR + DS:DR + 2 * DS]),
                (w_dt[DTROW:XROWS], I["dt_w"]), (b_dt[:], I["dt_b"]),
                (a_neg[:], I["A_logs"]), (d_skip[:], I["Dp"]), (w_out[:], I["out_w"]),
                (ln_g[:], I["ln_g"]), (ln_b[:], I["ln_b"]),
                (w1[:], I["w1"]), (b1[:], I["b1"]), (w2[:], I["w2"]), (b2_rows[:], I["b2"].to_broadcast([P, C])),
                (wr[:], I["wr"]), (br[:], I["br"].to_broadcast([P, 1])),
                (f_w1[:], I["f_w1"]), (f_b1[:], I["f_b1"]), (f_w2[:], I["f_w2"]), (f_b2[:], I["f_b2"]),
            ]
            row_loads = [(slice(QUAD * n, QUAD * n + DS), slice(DR, DR + DS)) for n in range(3)]
            row_loads.append((slice(DTROW, XROWS), slice(0, DR)))
            n_loads = len(loads) + len(row_loads)

            @block.sync
            def _(sp):
                with nc.allow_non_contiguous_dma(reason="weights, once"):
                    for dst, src in loads:
                        sp.dma_start(dst, src).then_inc(loaded, 16)
                    sp.wait_ge(zeroed, 1)
                    for dst, src in row_loads:
                        sp.dma_start(w_rows[:, :, :, dst], I["x_proj"][:, :, :, src]).then_inc(loaded, 16)
                sp.wait_ge(loaded, 16 * n_loads)

            @block.gpsimd
            def _(pool):
                pool.memset(w_rows[:], 0.0).then_inc(zeroed, 1)
                pool.memset(ident[:], 0.0).then_inc(zeroed, 1)
                pool.memset(below[:], 1.0).then_inc(zeroed, 1)
                pool.memset(pick[:], 0.0).then_inc(zeroed, 1)
                pool.memset(ones_row[:], 1.0)
                pool.memset(minus_half[:], -0.5)
                pool.memset(counts[:], 0.0)
                pool.memset(x_pad[:], 0.0)
                pool.wait_ge(zeroed, 4)
                pool.affine_select(out=ident[:], in_=ident[:], compare_op=ALU.not_equal, fill=1.0,
                                   base=0, pattern=[[-1, P]], channel_multiplier=1)
                pool.affine_select(out=below[:], in_=below[:], compare_op=ALU.is_gt, fill=0.0,
                                   base=0, pattern=[[-1, P]], channel_multiplier=1)
                for n in range(3):
                    if n:
                        pool.wait_ge(picked, n)
                    pool.affine_select(out=pick[:], in_=pick[:], compare_op=ALU.not_equal, fill=1.0,
                                       base=-QUAD * n, pattern=[[-1, DS]], channel_multiplier=1).then_inc(picked, 1)

            @block.scalar
            def _(act):
                act.wait_ge(loaded, 16 * n_loads)
                act.activation(a_neg[:], a_neg[:], ACT.Exp).then_inc(setup_exp, 1)

            @block.vector
            def _(dve):
                dve.wait_ge(loaded, 16 * n_loads)
                dve.tensor_scalar(bq[:], bq[:], SCALE, None, ALU.mult)
                dve.tensor_copy(wr_cols[:], wr[:].to_broadcast([C, P]))
                for r in range(DIRS):
                    for tap in range(KCONV):
                        dve.tensor_tensor(w_conv[:, r, tap, :], w_conv[:, r, tap, :], in_cols[:, r, :], ALU.mult)
                dve.wait_ge(setup_exp, 1)
                dve.tensor_scalar(a_neg[:], a_neg[:], -1.0, None, ALU.mult)

        x_loaded, stored = sem("x_loaded"), sem("stored")
        xt_made, xt_kept = sem("xt_made"), sem("xt_kept")
        q_made, k_made, v_made = sem("q_made"), sem("k_made"), sem("v_made")
        q_kept, k_kept, v_kept = sem("q_kept"), sem("k_kept"), sem("v_kept")
        scores_made, max_made, probs_made = sem("scores_made"), sem("max_made"), sem("probs_made")
        probs_turned, probs_kept = sem("probs_turned"), sem("probs_kept")
        attn_made, rinv_made, t1_made = sem("attn_made"), sem("rinv_made"), sem("t1_made")
        t1_moved = sem("t1_moved")
        ln_stats = [sem(f"ln_stats{n}") for n in range(3)]
        ln_var = [sem(f"ln_var{n}") for n in range(3)]
        ln_eps = [sem(f"ln_eps{n}") for n in range(3)]
        ln_rstd = [sem(f"ln_rstd{n}") for n in range(3)]
        ln_made = [sem(f"ln_made{n}") for n in range(3)]
        ln_turned = [sem(f"ln_turned{n}") for n in range(3)]
        ln_kept = [sem(f"ln_kept{n}") for n in range(3)]

        def two(name):
            return [sem(f"{name}{r}") for r in range(DIRS)]

        xc_made, xc_kept = two("xc_made"), two("xc_kept")
        z_made, z_kept = two("z_made"), two("z_kept")
        rows_made, rows_kept = two("rows_made"), two("rows_kept")
        c_made, c_kept = two("c_made"), two("c_kept")
        b_high, b_mid, b_low = two("b_high"), two("b_mid"), two("b_low")
        b_rest1, b_rest2 = two("b_rest1"), two("b_rest2")
        dt_made, dt_in, dt_exp, dt_log = two("dt_made"), two("dt_in"), two("dt_exp"), two("dt_log")
        dt_cut, dt_kept = two("dt_cut"), two("dt_kept")
        u_made = two("u_made")
        y_turned, y_skip, y_gated = two("y_turned"), two("y_skip"), two("y_gated")
        b_cast, b_cast_kept = sem("b_cast"), sem("b_cast_kept")
        dbx_made, da_made = sem("dbx_made"), sem("da_made")
        h_made, h_turned, y_added = sem("h_made"), sem("h_turned"), sem("y_added")
        m0_made, m0_kept = sem("m0_made"), sem("m0_kept")
        m1_made, m_kept = sem("m1_made"), sem("m_kept")
        hid1_made, hid1_kept, hid1_leaky = sem("hid1_made"), sem("hid1_kept"), sem("hid1_leaky")
        mlp_made, mt_made, b2_added = sem("mlp_made"), sem("mt_made"), sem("b2_added")
        t2_made, base_made = sem("t2_made"), sem("base_made")
        w_made, w_row_kept, w_turned, w_col_kept = (sem(n) for n in ("w_made", "w_row_kept", "w_turned", "w_col_kept"))
        compared, ranked, w_kept_made = sem("compared"), sem("ranked"), sem("w_kept_made")
        hid2_made, hid2_kept, ffn_made, t3_made = (sem(n) for n in ("hid2_made", "hid2_kept", "ffn_made", "t3_made"))
        out_turned, out_kept = sem("out_turned"), sem("out_kept")

        def turn(image, last, now, nxt):

            first_cast = LEAD_BC if now else ALL
            first_kept = LEAD_KEPT if now else ALL
            first_dbx = LEAD_DBX if now else ALL
            first_da = 1 if now else DIRS * DS
            end_step = ALL if now else 0

            def made_ahead(n):
                return n < ALL or nxt

            with nc.Block() as block:

                @block.sync
                def _(sp):
                    if nxt:
                        sp.dma_start(x_in, I["x"][image + 1]).then_inc(x_loaded, 16)
                    if last:
                        sp.wait_ge(out_kept, 1)
                        sp.dma_start(out[image - 1], out_s).then_inc(stored, 16)
                        sp.wait_ge(stored, 16)

                @block.tensor
                def _(pe):
                    def mm(o, a, b, first=True, last=True):
                        return nc.tensor.matmul(o, a, b, start=first, stop=last)

                    def flip(o, src):
                        return nc.tensor.transpose(o, src, ident[:])

                    def turn_h(n, part):
                        if part == 0:
                            pe.wait_ge(h_made, NH * (n + 1))
                        if n:
                            pe.wait_ge(y_added, QB * (n - 1) + 2 * (part + 1))
                        for b in range(2):
                            for half in range(NH):
                                t = flip(ps[:, HB + part, (NH * b + half) * P:(NH * b + half + 1) * P],
                                         h[:, n % 2, half, (2 * part + b) * P:(2 * part + b + 1) * P])
                        t.then_inc(h_turned, 1)

                    def cast_b(n):
                        r, (s, c) = n // STEPS % DIRS, divmod(n % STEPS, NCH)
                        if n % STEPS == 0:
                            pe.wait_ge(b_low[r], 1)
                        if n > first_cast or now:
                            pe.wait_ge(b_cast_kept, n - first_kept)
                        mm(ps[:, BB, :], pick[:, s:s + 1].to_broadcast([BROWS, P]), b_parts[:, r, cols(c)]
                           ).then_inc(b_cast, 1)

                    def tokens(r, tap, c):
                        if r == 0:
                            return x_pad[:, tap + c * BANK:tap + (c + 1) * BANK]
                        at = T + 2 * PAD - 1 - tap - c * BANK
                        return x_pad[:, at:at - BANK:-1]

                    def conv(r, part):
                        half, c, pair = part // (2 * NCH), part // 2 % NCH, part % 2
                        bank = (X, Y)[half] + c
                        for tap in (2 * pair, 2 * pair + 1):
                            t = mm(ps[:, bank, :], w_conv[:, r, tap, half * P:(half + 1) * P], tokens(r, tap, c),
                                   tap == 0, tap == KCONV - 1)
                        if c == NCH - 1 and pair == 1:
                            t.then_inc(xc_made[r], 1)

                    def gate(r, half, bank):
                        for c in range(NCH):
                            t = mm(ps[:, bank + c, :], w_z[:, r, half * P:(half + 1) * P], tokens(r, PAD, c))
                        t.then_inc(z_made[r], 1)

                    def turn_y(r, half):
                        for i in range(NB):
                            t = flip(banks((X, Y)[half])[:, i * P:(i + 1) * P], y_tok[:, i, half * P:(half + 1) * P])
                        t.then_inc(y_turned[r], 1)

                    def project(r, part, bank, made):
                        for b in range(QB):
                            i = QB * part + b
                            for half in range(NH):
                                t = mm(ps[:, bank, b * C:(b + 1) * C], xc[:, r, half, i * P:(i + 1) * P],
                                       w_out[:, r, half, :], half == 0, half == NH - 1)
                        t.then_inc(made, 1)

                    def turn_blocks(src, bank):
                        for i in range(NB):
                            t = flip(banks(bank)[:, i * P:(i + 1) * P], src[:, i, :])
                        return t

                    def before_scan(g, r):
                        if g in AT_CONV[r]:
                            part = AT_CONV[r].index(g)
                            if part == 0 and r == 1:
                                pe.wait_ge(z_kept[0], NH)
                            if part == 0 and r == 0:
                                pe.wait_ge(ln_kept[0], 1)
                                if now:
                                    pe.wait_ge(m0_kept, 1)
                            conv(r, part)
                        if g in AT_ROWS[r]:
                            c = AT_ROWS[r].index(g)
                            if c == 0:
                                pe.wait_ge(xc_kept[r], NH)
                                if r == 1 and last:
                                    pe.wait_ge(m_kept, 2)
                                if r == 0:
                                    pe.wait_ge(t1_made, NB)
                            else:
                                pe.wait_ge(rows_kept[r], c)
                            for half in range(NH):
                                t = mm(ps[0:XROWS, Z, :], w_rows[:, r, half, :], xc[:, r, half, cols(c)],
                                       half == 0, half == NH - 1)
                            t.then_inc(rows_made[r], 1)
                        if g == AT_C[r]:
                            pe.wait_ge(rows_kept[r], NCH)
                            for i in range(NB):
                                for half in range(NH):
                                    t = mm(ps[:, Z, i * DS:(i + 1) * DS], xc[:, r, half, i * P:(i + 1) * P],
                                           w_c[:, r, half, :], half == 0, half == NH - 1)
                            t.then_inc(c_made[r], 1)
                        if g in AT_DT[r]:
                            half = AT_DT[r].index(g)
                            pe.wait_ge(rows_kept[r], NCH)
                            if r == 1 and last:
                                if half == 0:
                                    pe.wait_ge(hid1_kept, HM)
                                else:
                                    pe.wait_ge(t2_made, 1)
                            for c in range(NCH):
                                t = mm(ps[:, (X, Y)[half] + c, :], w_dt[DTROW:XROWS, r, half * P:(half + 1) * P],
                                       rows[DTROW:XROWS, cols(c)])
                            t.then_inc(dt_made[r], 1)

                    def finish_last(g):
                        if g in AT_YT[1]:
                            turn_y(1, AT_YT[1].index(g))
                        if g in AT_M1:
                            part = AT_M1.index(g)
                            pe.wait_ge(y_gated[1], NH * (part + 1))
                            if part:
                                pe.wait_ge(m_kept, part)
                            project(1, part, Z, m1_made)
                        if g == LN_TURN[1]:
                            pe.wait_ge(ln_made[1], NB)
                            if now:
                                pe.wait_ge(xc_kept[1], NH)
                            turn_blocks(m_normed, X).then_inc(ln_turned[1], 1)
                        if g in AT_W1:
                            o = AT_W1.index(g)
                            pe.wait_ge(ln_kept[1], 1)
                            for c in range(NCH):
                                t = mm(ps[:, (Y, X)[o] + c, :], w1[:, o * P:(o + 1) * P], h1[:, cols(c)])
                            t.then_inc(hid1_made, 1)
                        if g in AT_W2:
                            part = AT_W2.index(g)
                            pe.wait_ge(hid1_leaky, HM)
                            for b in range(QB):
                                i = QB * part + b
                                for o in range(HM):
                                    t = mm(ps[:, Y + part, b * C:(b + 1) * C], hid[:, o, i * P:(i + 1) * P], w2[:, o, :],
                                           o == 0, o == HM - 1)
                            t.then_inc(mlp_made, 1)
                        if g == LN_TURN[2]:
                            pe.wait_ge(ln_made[2], NB)
                            if now:
                                pe.wait_ge(dt_exp[1], 1)
                            turn_blocks(n2, X).then_inc(ln_turned[2], 1)
                        if g == AT_W:
                            pe.wait_ge(ln_kept[2], 1)
                            if now:
                                pe.wait_ge(dt_exp[1], 2)
                            for c in range(NCH):
                                t = mm(ps[:, Y + c, :], wr_cols[:], n2c[:, cols(c)])
                            t.then_inc(w_made, 1)
                        if g in AT_HID:
                            o = AT_HID.index(g)
                            if o == 1:
                                pe.wait_ge(w_row_kept, 1)
                            if o >= 2:
                                pe.wait_ge(hid2_kept, o - 1)
                            for c in range(NCH):
                                t = mm(ps[:, (X, Y)[o % 2] + c, :], f_w1[:, o * P:(o + 1) * P], n2c[:, cols(c)])
                            t.then_inc(hid2_made, 1)
                        if g == AT_WTURN:
                            pe.wait_ge(w_row_kept, 1)
                            if now:
                                pe.wait_ge(c_kept[1], 1)
                            for i in range(NB):
                                t = nc.tensor.transpose(ps[:, Z, i:i + 1], w_row[0:1, i * P:(i + 1) * P],
                                                        ident[0:1, 0:1])
                            t.then_inc(w_turned, 1)
                        if AT_FFN <= g < AT_FFN + NB // 2:
                            if g == AT_FFN:
                                pe.wait_ge(hid2_kept, HF)
                            for i in (2 * (g - AT_FFN), 2 * (g - AT_FFN) + 1):
                                for o in range(HF):
                                    mm(banks(X)[:, i * C:(i + 1) * C], hid[:, o, i * P:(i + 1) * P], f_w2[:, o, :],
                                       o == 0, False)
                                t = mm(banks(X)[:, i * C:(i + 1) * C], ones_row[:], f_b2[:], False, True)
                            t.then_inc(ffn_made, 1)
                        if g == AT_OUT:
                            pe.wait_ge(t3_made, NB)
                            turn_blocks(res, Y).then_inc(out_turned, 1)

                    def attend_next(g):
                        if g == AT_XT:
                            pe.wait_ge(x_loaded, 16)
                            if last:
                                pe.wait_ge(y_skip[1], 1)
                            for i in range(NB):
                                t = flip(banks(X)[:, i * C:(i + 1) * C], x_in[:, i * P:(i + 1) * P])
                            t.then_inc(xt_made, 1)
                        for at, w, bank, made in ((AT_Q, wq, Y, q_made), (AT_K, wk, X, k_made)):
                            if g == at:
                                if g == AT_Q and last:
                                    pe.wait_ge(y_skip[1], 2)
                                if g == AT_K:
                                    pe.wait_ge(xt_kept, 1)
                                for c in range(NCH):
                                    t = mm(ps[:, bank + c, :], w[:], x_in[:, cols(c)])
                                t.then_inc(made, 1)
                        if g == AT_V:
                            pe.wait_ge(q_kept, 1)
                            for i in range(NB):
                                t = mm(banks(Y)[:, i * C:(i + 1) * C], x_in[:, i * P:(i + 1) * P], wv[:])
                            t.then_inc(v_made, 1)
                        if g in AT_S:
                            i = AT_S.index(g)
                            if i == 0:
                                pe.wait_ge(k_kept, 1)
                                if last:
                                    pe.wait_ge(t3_made, NB)
                            else:
                                pe.wait_ge(probs_made, i)
                                if now and i == 1:
                                    pe.wait_ge(y_skip[0], 1)
                            for c in range(NCH):
                                t = mm(ps[:, X + c, :], q[:, i * P:(i + 1) * P], k[:, cols(c)])
                            t.then_inc(scores_made, 1)
                        if g in AT_PT:
                            i = AT_PT.index(g)
                            pe.wait_ge(probs_made, i + 1)
                            if i == 0:
                                pe.wait_ge(v_kept, 1)
                                if now:
                                    pe.wait_ge(y_skip[0], 2)
                            else:
                                pe.wait_ge(probs_kept, i)
                            for b in range(NB):
                                t = flip(banks(Y)[:, b * P:(b + 1) * P], probs[:, b * P:(b + 1) * P])
                            t.then_inc(probs_turned, 1)
                        if g in AT_PV:
                            i = AT_PV.index(g)
                            pe.wait_ge(probs_kept, i + 1)
                            if i == 0 and last:
                                pe.wait_ge(w_col_kept, 1)
                            if i:
                                pe.wait_ge(t1_made, i)
                            for b in range(NB):
                                t = mm(ps[:, Z, 0:C], probs_t[:, b, :], v_tok[:, b, :], b == 0, b == NB - 1)
                            t.then_inc(attn_made, 1)
                        if g == LN_TURN[0]:
                            pe.wait_ge(ln_made[0], NB)
                            pe.wait_ge(probs_kept, NB)
                            if now:
                                pe.wait_ge(z_kept[1], NH)
                            turn_blocks(x_tok, Y).then_inc(ln_turned[0], 1)

                    def aside(g):
                        if last:
                            finish_last(g)
                        if nxt:
                            attend_next(g)
                            before_scan(g, 0)
                        if now:
                            before_scan(g, 1)
                            if g == AT_YT[0][0]:
                                pe.wait_ge(y_added, QB * STEPS)
                                if nxt:
                                    pe.wait_ge(probs_made, 1)
                                if last:
                                    pe.wait_ge(out_kept, 1)
                                turn_y(0, 0)
                                turn_y(0, 1)
                            for r in range(DIRS):
                                if g in AT_Z[r]:
                                    half = AT_Z[r].index(g)
                                    if r == 0:
                                        if last:
                                            pe.wait_ge(y_skip[1], half + 1)
                                        if nxt:
                                            pe.wait_ge((k_kept, v_kept)[half], 1)
                                    elif nxt:
                                        pe.wait_ge((probs_made, probs_kept)[half], NB)
                                    else:
                                        pe.wait_ge(y_skip[0], half + 1)
                                    gate(r, half, (X, Y)[half])
                            if g in AT_M0:
                                part = AT_M0.index(g)
                                pe.wait_ge(z_kept[1], NH)
                                pe.wait_ge(y_gated[0], NH * NCH)
                                project(0, part, X + part, m0_made)

                    for n in range(end_step):
                        turn_h(n, 0)
                        aside(2 * n)
                        turn_h(n, 1)
                        if made_ahead(n + LEAD_BC):
                            cast_b(n + LEAD_BC)
                        aside(2 * n + 1)
                    if not now:
                        for g in range(2 * ALL):
                            aside(g)
                        if nxt:
                            for n in range(LEAD_BC):
                                cast_b(ALL + n)

                @block.scalar
                def _(act):
                    def decay(n):
                        s, half = divmod(n, NH)
                        r = s // DS % DIRS
                        if s % DS == 0:
                            act.wait_ge(dt_kept[r], half + 1)
                        if now and s >= 2:
                            act.wait_ge(h_made, NH * (NCH * (s - 1) - 1) + half + 1)
                        act.activation(da[:, s % 2, half, :], dt[:, r, half, :], ACT.Exp,
                                       scale=a_neg[:, r, half, s % DS:s % DS + 1]).then_inc(da_made, 1)

                    def keep_b(n):
                        if n >= first_cast:
                            act.wait_ge(b_cast, n - first_cast + 1)
                        if n - 2 >= first_dbx:
                            act.wait_ge(dbx_made, n - 2 - first_dbx + 1)
                        act.activation(b_all[:, n % 2, :], ps[:, BB, :], ACT.Copy).then_inc(b_cast_kept, 1)

                    def before_scan(g, r):
                        if g == AT_XC[r]:
                            if r == 1 and last:
                                act.wait_ge(m1_made, 2)
                            if r == 0 and now:
                                act.wait_ge(m0_made, 2)
                            for half in range(NH):
                                act.wait_ge(xc_made[r], half + 1)
                                act.activation(xc[:, r, half, :], banks((X, Y)[half]), ACT.Silu,
                                               bias=conv_b[:, r, half:half + 1]).then_inc(xc_kept[r], 1)
                        if g in AT_ROWKEEP[r]:
                            c = AT_ROWKEEP[r].index(g)
                            act.wait_ge(rows_made[r], c + 1)
                            if r == 0 and now and c == 0:
                                act.wait_ge(dt_made[1], NH)
                                act.wait_ge(b_low[1], 1)
                            act.activation(rows[:, cols(c)], ps[0:XROWS, Z, :], ACT.Copy).then_inc(rows_kept[r], 1)
                        if g == AT_BHI[r]:
                            act.wait_ge(rows_kept[r], NCH)
                            if r == 0 and now:
                                act.wait_ge(b_cast, STEPS - first_cast)
                            act.activation(b_parts[:, r, :], rows[0:BROWS, :], ACT.Copy).then_inc(b_high[r], 1)
                        if g == AT_BMID[r]:
                            act.wait_ge(b_rest1[r], 1)
                            act.activation(b_parts[QUAD:2 * QUAD, r, :], rows[QUAD:2 * QUAD, :], ACT.Copy
                                           ).then_inc(b_mid[r], 1)
                            act.activation(b_parts[2 * QUAD:BROWS, r, :], rows[2 * QUAD:BROWS, :], ACT.Copy
                                           ).then_inc(b_mid[r], 1)
                        if g == AT_BLO[r]:
                            act.wait_ge(b_rest2[r], 1)
                            act.activation(b_parts[2 * QUAD:BROWS, r, :], rows[2 * QUAD:BROWS, :], ACT.Copy
                                           ).then_inc(b_low[r], 1)
                        if g == AT_CKEEP[r]:
                            act.wait_ge(c_made[r], 1)
                            if r == 0 and now:
                                act.wait_ge(y_added, QB * STEPS)
                            act.activation(c_tok[:, r, :, :].rearrange("p b s -> p (b s)"), ps[:, Z, 0:NB * DS], ACT.Copy
                                           ).then_inc(c_kept[r], 1)
                        if g in AT_DTEXP[r]:
                            half = AT_DTEXP[r].index(g)
                            act.wait_ge(dt_made[r], half + 1)
                            bank = banks((X, Y)[half])
                            if r == 0 and now and half == 0:
                                act.wait_ge(dbx_made, STEPS - first_dbx)
                            act.activation(dt[:, r, half, :], bank, ACT.Identity, bias=b_dt[:, r, half:half + 1]
                                           ).then_inc(dt_in[r], 1)
                            act.activation(u[:, r, half, :], bank, ACT.Exp, bias=b_dt[:, r, half:half + 1]
                                           ).then_inc(dt_exp[r], 1)
                        if g in AT_LOG[r]:
                            half = AT_LOG[r].index(g)
                            act.wait_ge(dt_cut[r], half + 1)
                            act.activation(u[:, r, half, :], u[:, r, half, :], ACT.Ln, bias=1.0).then_inc(dt_log[r], 1)

                    def finish_last(g):
                        if g == LN_KEEP[1]:
                            act.wait_ge(ln_turned[1], 1)
                            act.activation(h1, banks(X), ACT.Identity, bias=ln_b[:], scale=ln_g[:]
                                           ).then_inc(ln_kept[1], 1)
                        if g in AT_HID1:
                            o = AT_HID1.index(g)
                            act.wait_ge(hid1_made, o + 1)
                            act.activation(hid[:, o, :], banks((Y, X)[o]), ACT.Identity,
                                           bias=b1[:, o:o + 1]).then_inc(hid1_kept, 1)
                        if g == LN_KEEP[2]:
                            act.wait_ge(ln_turned[2], 1)
                            act.activation(n2c, banks(X), ACT.Copy).then_inc(ln_kept[2], 1)
                        if g == AT_WKEEP:
                            act.wait_ge(w_made, 1)
                            if nxt:
                                act.wait_ge(v_made, 1)
                            act.activation(w_row, banks(Y), ACT.Identity, bias=br[:]).then_inc(w_row_kept, 1)
                        if g in AT_GELU:
                            for o in (2 * AT_GELU.index(g), 2 * AT_GELU.index(g) + 1):
                                act.wait_ge(hid2_made, o + 1)
                                act.activation(hid[:, o, :], banks((X, Y)[o % 2]), ACT.Gelu_apprx_tanh,
                                               bias=f_b1[:, o:o + 1]).then_inc(hid2_kept, 1)
                        if g == AT_OUTKEEP:
                            act.wait_ge(out_turned, 1)
                            act.activation(out_s, banks(Y), ACT.Copy).then_inc(out_kept, 1)

                    def attend_next(g):
                        if g == AT_QKEEP:
                            act.wait_ge(q_made, 1)
                            act.activation(q[:], banks(Y), ACT.Identity, bias=bq[:], scale=SCALE).then_inc(q_kept, 1)
                        if g == AT_KKEEP:
                            act.wait_ge(k_made, 1)
                            act.activation(k[:], banks(X), ACT.Identity, bias=bk[:]).then_inc(k_kept, 1)
                        if g == AT_VKEEP:
                            act.wait_ge(v_made, 1)
                            act.activation(v_tok[:], blocks(Y), ACT.Copy).then_inc(v_kept, 1)
                        if g in AT_EXP:
                            i = AT_EXP.index(g)
                            act.wait_ge(max_made, i + 1)
                            if i == 0 and last:
                                act.wait_ge(compared, 3 * NB - 1)
                            if i:
                                act.wait_ge(probs_turned, i)
                            act.activation(probs, banks(X), ACT.Exp, bias=nmax[:, i:i + 1],
                                           accum_out=rowsum[:, i:i + 1]).then_inc(probs_made, 1)
                        if g in AT_PTKEEP:
                            i = AT_PTKEEP.index(g)
                            act.wait_ge(probs_turned, i + 1)
                            if i:
                                act.wait_ge(attn_made, i)
                            act.activation(probs_t, blocks(Y), ACT.Copy).then_inc(probs_kept, 1)
                        if g == LN_KEEP[0]:
                            act.wait_ge(ln_turned[0], 1)
                            act.activation(x_pad[:, PAD:PAD + T], banks(Y), ACT.Copy).then_inc(ln_kept[0], 1)

                    def aside(g):
                        if last:
                            finish_last(g)
                        if nxt:
                            attend_next(g)
                            before_scan(g, 0)
                        if now:
                            before_scan(g, 1)
                            for r in range(DIRS):
                                if g == AT_ZKEEP[r]:
                                    if last or r == 1:
                                        act.wait_ge(y_gated[1 - r], NH * NCH)
                                    for half in range(NH):
                                        act.wait_ge(z_made[r], half + 1)
                                        act.activation(sz[:, half, :], banks((X, Y)[half]), ACT.Silu
                                                       ).then_inc(z_kept[r], 1)
                            if g == AT_T1OLD:
                                if last:
                                    act.wait_ge(mt_made, 2)
                                act.activation(t1_old[:], t1[:], ACT.Copy).then_inc(t1_moved, 1)
                            if g == AT_M0KEEP:
                                act.wait_ge(m0_made, 2)
                                if last:
                                    act.wait_ge(m_kept, 2)
                                act.activation(m0[:], blocks(X), ACT.Copy).then_inc(m0_kept, 1)

                    for n in range(end_step):
                        if n // NCH + 1 < DIRS * DS or nxt:
                            decay(n + NH)
                        aside(2 * n)
                        if made_ahead(n + LEAD_KEPT):
                            keep_b(n + LEAD_KEPT)
                        aside(2 * n + 1)
                    if not now:
                        for g in range(2 * ALL):
                            aside(g)
                        if nxt:
                            for half in range(NH):
                                decay(NH * DIRS * DS + half)
                            for n in range(LEAD_KEPT):
                                keep_b(ALL + n)

                @block.gpsimd
                def _(pool):
                    def times_b(n):
                        r, (s, c) = n // STEPS % DIRS, divmod(n % STEPS, NCH)
                        if s == 0 and n >= STEPS:
                            pool.wait_ge(u_made[r], NH * (c + 1))
                        if n >= first_kept:
                            pool.wait_ge(b_cast_kept, n - first_kept + 1)
                        if now and n >= 2:
                            pool.wait_ge(h_made, NH * (n - 1))
                        pool.tensor_tensor(dbx[:, n % 2, :, :], u[:, r, :, cols(c)],
                                           b_all[:, n % 2, :].unsqueeze(1).to_broadcast([P, NH, BANK]), ALU.mult
                                           ).then_inc(dbx_made, 1)

                    def inverse_deviation(n):
                        pool.wait_ge(ln_var[n], NB)
                        pool.tensor_scalar(var_eps[:], mean_var[:, :, 1], EPS, None, ALU.add).then_inc(ln_eps[n], 1)
                        pool.wait_ge(ln_eps[n], 1)
                        pool.tensor_tensor(rstd[:], var_eps[:], minus_half[:], ALU.pow).then_inc(ln_rstd[n], 1)

                    def half_sum(o, a, b, part):
                        some = slice(QB * part, QB * (part + 1))
                        return pool.tensor_tensor(o[:, some, :], a[:, some, :], b[:, some, :], ALU.add)

                    def make_u(r, part):
                        c, half = divmod(part, NH)
                        pool.wait_ge(dt_kept[r], half + 1)
                        pool.tensor_tensor(u[:, r, half, cols(c)], dt[:, r, half, cols(c)], xc[:, r, half, cols(c)],
                                           ALU.mult).then_inc(u_made[r], 1)

                    def make_gated(r, part):
                        c, half = divmod(part, NH)
                        pool.wait_ge(y_skip[r], half + 1)
                        pool.tensor_tensor(xc[:, r, half, cols(c)], xc[:, r, half, cols(c)], sz[:, half, cols(c)],
                                           ALU.mult).then_inc(y_gated[r], 1)

                    def aside(step):
                        if last:
                            if STEP_GATE[1] <= step < STEP_GATE[1] + NH * NCH:
                                make_gated(1, step - STEP_GATE[1])
                            if step in STEP_MT:
                                part = STEP_MT.index(step)
                                pool.wait_ge(m_kept, part + 1)
                                half_sum(res, m, t1_old, part).then_inc(mt_made, 1)
                            if step in STEP_B2:
                                part = STEP_B2.index(step)
                                pool.wait_ge(mt_made, part + 1)
                                some = slice(QB * part, QB * (part + 1))
                                pool.tensor_tensor(res[:, some, :], res[:, some, :],
                                                   b2_rows[:].unsqueeze(1).to_broadcast([P, QB, C]), ALU.add
                                                   ).then_inc(b2_added, 1)
                            for n in (1, 2):
                                if step == STEP_LN[n]:
                                    inverse_deviation(n)
                            if step in STEP_BASE:
                                part = STEP_BASE.index(step)
                                pool.wait_ge(ln_made[2], NB)
                                half_sum(res, res, n2, part).then_inc(base_made, 1)
                        if nxt:
                            if step == STEP_LN[0]:
                                inverse_deviation(0)
                            for part in range(NH * NCH):
                                if step == STEP_U[0][part]:
                                    make_u(0, part)
                        if now:
                            if STEP_GATE[0] <= step < STEP_GATE[0] + NH * NCH:
                                make_gated(0, step - STEP_GATE[0])
                            for part in range(NH * NCH):
                                if step == STEP_U[1][part]:
                                    make_u(1, part)

                    for n in range(end_step):
                        if made_ahead(n + LEAD_DBX):
                            times_b(n + LEAD_DBX)
                        aside(n)
                    if not now:
                        for step in range(ALL):
                            aside(step)
                        if nxt:
                            times_b(ALL)

                @block.vector
                def _(dve):
                    def scan(n):
                        s, c = divmod(n, NCH)
                        for half in range(NH):
                            if n:
                                dve.wait_ge(h_made, NH * (n - 1) + half + 1)
                            if c == 0:
                                if s >= first_da:
                                    dve.wait_ge(da_made, NH * (s - first_da) + half + 1)
                                before = 0.0
                            else:
                                before = h[:, (n - 1) % 2, half, BANK - 1:BANK]
                            if n >= first_dbx and half == 0:
                                dve.wait_ge(dbx_made, n - first_dbx + 1)
                            dve.tensor_tensor_scan(h[:, n % 2, half, :], da[:, s % 2, half, cols(c)],
                                                   dbx[:, n % 2, half, :], before, ALU.mult, ALU.add
                                                   ).then_inc(h_made, 1)

                    def add_y(n, part):
                        r, (s, c) = n // STEPS, divmod(n % STEPS, NCH)
                        dve.wait_ge(h_turned, 2 * n + part + 1)
                        if s == 0 and c == 0 and part == 0 and (r == 1 or last):
                            dve.wait_ge(y_turned[1 - r], NH)
                        for b in (2 * part, 2 * part + 1):
                            i = QB * c + b
                            src = ps[:, HB + part, (b % 2) * DI:(b % 2 + 1) * DI]
                            weight = c_tok[:, r, i, s:s + 1]
                            if s == 0:
                                dve.tensor_scalar(y_tok[:, i, :], src, weight, None, ALU.mult).then_inc(y_added, 1)
                            else:
                                dve.wait_ge(y_added, QB * (n - NCH) + b + 1)
                                dve.scalar_tensor_tensor(y_tok[:, i, :], src, weight, y_tok[:, i, :],
                                                         ALU.mult, ALU.add).then_inc(y_added, 1)

                    def layer_norm(g, n):
                        src, dst = ln_tile[n]
                        if g == LN_STATS[n]:
                            if n == 0:
                                dve.wait_ge(t1_made, NB)
                            if n == 1:
                                dve.wait_ge(m_kept, 2)
                            if n == 2:
                                dve.wait_ge(t2_made, 1)
                            for i in range(NB):
                                dve.bn_stats(stats[:, i, :], src[:, i, :]).then_inc(ln_stats[n], 1)
                        if g == LN_AGGR[n]:
                            for i in range(NB):
                                dve.wait_ge(ln_stats[n], i + 1)
                                dve.bn_aggr(mean_var[:, i, :], stats[:, i, :]).then_inc(ln_var[n], 1)
                        if g == LN_APPLY[n]:
                            dve.wait_ge(ln_rstd[n], 1)
                            if n == 2:
                                dve.wait_ge(mt_made, 2)
                            for i in range(NB):
                                dve.tensor_scalar(dst[:, i, :], src[:, i, :], mean_var[:, i, 0:1], rstd[:, i:i + 1],
                                                  ALU.subtract, ALU.mult).then_inc(ln_made[n], 1)

                    def skip(g, r):
                        if g in AT_SKIP[r]:
                            half = AT_SKIP[r].index(g)
                            dve.wait_ge(y_turned[r], half + 1)
                            dve.scalar_tensor_tensor(xc[:, r, half, :], xc[:, r, half, :], d_skip[:, r, half:half + 1],
                                                     banks((X, Y)[half]), ALU.mult, ALU.add).then_inc(y_skip[r], 1)

                    def before_scan(g, r):
                        if g == AT_BR1[r]:
                            dve.wait_ge(b_high[r], 1)
                            dve.tensor_tensor(rows[0:BROWS, :], rows[0:BROWS, :], b_parts[:, r, :], ALU.subtract
                                              ).then_inc(b_rest1[r], 1)
                        if g == AT_BR2[r]:
                            dve.wait_ge(b_mid[r], 2)
                            low = slice(2 * QUAD, BROWS)
                            dve.tensor_tensor(rows[low, :], rows[low, :], b_parts[low, r, :], ALU.subtract
                                              ).then_inc(b_rest2[r], 1)
                        if g in AT_CUT[r]:
                            half = AT_CUT[r].index(g)
                            dve.wait_ge(dt_exp[r], half + 1)
                            dve.tensor_scalar(u[:, r, half, :], u[:, r, half, :], EXP_MAX, None, ALU.min
                                              ).then_inc(dt_cut[r], 1)
                        if g in AT_DTMAX[r]:
                            half = AT_DTMAX[r].index(g)
                            dve.wait_ge(dt_log[r], half + 1)
                            dve.tensor_tensor(dt[:, r, half, :], dt[:, r, half, :], u[:, r, half, :], ALU.max
                                              ).then_inc(dt_kept[r], 1)

                    def finish_last(g):
                        skip(g, 1)
                        if g in AT_MSUM:
                            part = AT_MSUM.index(g)
                            some = slice(QB * part, QB * (part + 1))
                            dve.wait_ge(m1_made, part + 1)
                            dve.tensor_tensor(m[:, some, :], by_block(ps[:, Z, :]), m0[:, some, :], ALU.add
                                              ).then_inc(m_kept, 1)
                        layer_norm(g, 1)
                        if g in AT_LEAKY:
                            o = AT_LEAKY.index(g)
                            dve.wait_ge(hid1_kept, o + 1)
                            dve.scalar_tensor_tensor(hid[:, o, :], hid[:, o, :], SLOPE, hid[:, o, :],
                                                     ALU.mult, ALU.max).then_inc(hid1_leaky, 1)
                        if g == AT_T2:
                            dve.wait_ge(b2_added, 2)
                            dve.wait_ge(mlp_made, 2)
                            dve.tensor_tensor(res[:], blocks(Y), res[:], ALU.add).then_inc(t2_made, 1)
                        layer_norm(g, 2)
                        if g == AT_WCOL:
                            dve.wait_ge(w_turned, 1)
                            dve.tensor_copy(w_col[:], ps[:, Z, 0:NB]).then_inc(w_col_kept, 1)
                        if AT_RANK <= g < AT_RANK + NB:
                            i = g - AT_RANK
                            if i == 0:
                                dve.wait_ge(w_col_kept, 1)
                                dve.wait_ge(w_row_kept, 1)
                                dve.wait_ge(base_made, 2)
                            done = max(3 * i - 1, 0)
                            parts = [(2, slice(i * P, (i + 1) * P)), (1, slice(i * P, T))]
                            if i:
                                parts.append((0, slice(0, i * P)))
                            for kind, some in parts:
                                if done:
                                    dve.wait_ge(compared, done)
                                if kind == 2:
                                    t = dve.scalar_tensor_tensor(junk[:, some], w_row[:, some], w_col[:, i:i + 1],
                                                                 below[:], ALU.is_equal, ALU.mult,
                                                                 accum_out=counts[:, i, 2:3])
                                else:
                                    t = dve.tensor_scalar(junk[:, some], w_row[:, some], w_col[:, i:i + 1], None,
                                                          (ALU.is_ge, ALU.is_gt)[kind], ALU.add,
                                                          accum_out=counts[:, i, kind:kind + 1])
                                t.then_inc(compared, 1)
                                done += 1
                        if g == AT_WK:
                            dve.wait_ge(compared, 3 * NB - 1)
                            dve.tensor_reduce(rank[:], counts[:], AX.X, ALU.add).then_inc(ranked, 1)
                            dve.wait_ge(ranked, 1)
                            dve.scalar_tensor_tensor(w_kept[:], rank[:], float(KEPT), w_col[:], ALU.is_lt, ALU.mult
                                                     ).then_inc(w_kept_made, 1)
                        if g in AT_T3:
                            part = AT_T3.index(g)
                            if part == 0:
                                dve.wait_ge(w_kept_made, 1)
                            dve.wait_ge(ffn_made, 2 * (part + 1))
                            for i in range(QB * part, QB * (part + 1)):
                                dve.scalar_tensor_tensor(res[:, i, :], blocks(X)[:, i, :], w_kept[:, i:i + 1],
                                                         res[:, i, :], ALU.mult, ALU.add).then_inc(t3_made, 1)

                    def attend_next(g):
                        if g == AT_XTOK:
                            dve.wait_ge(xt_made, 1)
                            dve.tensor_tensor(x_tok[:], blocks(X), bv_rows[:].unsqueeze(1).to_broadcast([P, NB, C]),
                                              ALU.add).then_inc(xt_kept, 1)
                        if g in AT_MAX:
                            i = AT_MAX.index(g)
                            dve.wait_ge(scores_made, i + 1)
                            dve.tensor_reduce(nmax[:, i:i + 1], banks(X), AX.X, ALU.max, negate=True
                                              ).then_inc(max_made, 1)
                        if g in AT_T1:
                            i = AT_T1.index(g)
                            if i == 0:
                                if now:
                                    dve.wait_ge(t1_moved, 1)
                                dve.wait_ge(xt_kept, 1)
                            dve.wait_ge(probs_made, i + 1)
                            dve.reciprocal(rinv[:, i:i + 1], rowsum[:, i:i + 1]).then_inc(rinv_made, 1)
                            dve.wait_ge(rinv_made, i + 1)
                            dve.wait_ge(attn_made, i + 1)
                            dve.scalar_tensor_tensor(t1[:, i, :], ps[:, Z, 0:C], rinv[:, i:i + 1], x_tok[:, i, :],
                                                     ALU.mult, ALU.add).then_inc(t1_made, 1)
                        layer_norm(g, 0)

                    def aside(g):
                        if last:
                            finish_last(g)
                        if nxt:
                            attend_next(g)
                            before_scan(g, 0)
                        if now:
                            before_scan(g, 1)
                            skip(g, 0)

                    for n in range(end_step):
                        scan(n)
                        if n:
                            add_y(n - 1, 0)
                        aside(2 * n)
                        if n:
                            add_y(n - 1, 1)
                        aside(2 * n + 1)
                    if now:
                        add_y(ALL - 1, 0)
                        add_y(ALL - 1, 1)
                    else:
                        for g in range(2 * ALL):
                            aside(g)

            nums = [s.num for s in turn_sems]
            nc.all_engine_barrier(sems_to_clear=range(min(nums), max(nums) + 1))

        turn(-1, last=False, now=False, nxt=True)
        turn(0, last=False, now=True, nxt=True)
        with nc.Fori(1, B - 1) as image:
            turn(image, last=True, now=True, nxt=True)
        turn(B - 1, last=True, now=True, nxt=False)
        turn(B, last=True, now=False, nxt=False)


def kernel(**inputs):
    import concourse.bacc as _bacc
    from concourse import mybir as _mybir
    from concourse.bass_utils import run_bass_kernel_spmd as _run

    a = {k: np.asarray(v) for k, v in inputs.items()}
    P = 128

    def columns(v):
        return np.moveaxis(v.reshape(*v.shape[:-1], v.shape[-1] // P, P), -1, 0)

    x = a["x"]
    B, C, H, W = x.shape
    m = {k.removeprefix("L1_attn_"): v for k, v in a.items() if k.startswith("L1_attn_")}
    f = {k.removeprefix("L1_ffn_"): v for k, v in a.items() if k.startswith("L1_ffn_")}
    DIRS, DI, KCONV = m["conv_w"].shape
    laid = {
        "x": x.reshape(B, C, H * W),
        "wq": a["L0_conv_Wq"].T, "wk": a["L0_conv_Wk"].T, "wv": a["L0_conv_Wv"].T,
        "bq": a["L0_conv_bq"].reshape(C, 1), "bk": a["L0_conv_bk"].reshape(C, 1),
        "bv": a["L0_conv_bv"].reshape(1, C),
        "in_proj": m["in_proj_w"].transpose(0, 2, 1),
        "conv_rows": m["conv_w"].transpose(0, 2, 1).reshape(1, -1),
        "conv_b": columns(m["conv_b"]),
        "x_proj": columns(m["x_proj_w"]).transpose(0, 1, 3, 2),
        "dt_w": m["dt_proj_w"].transpose(2, 0, 1),
        "dt_b": columns(m["dt_proj_b"]),
        "A_logs": columns(m["A_log"].transpose(0, 2, 1)).transpose(0, 1, 3, 2),
        "Dp": columns(m["Dp"]),
        "out_w": columns(m["out_proj_w"]).transpose(0, 1, 3, 2),
        "ln_g": m["ln_g"].reshape(C, 1), "ln_b": m["ln_b"].reshape(C, 1),
        "w1": m["w1"].T, "b1": columns(m["b1"]),
        "w2": columns(m["w2"]).transpose(0, 2, 1), "b2": m["b2"].reshape(1, C),
        "wr": f["wr"].reshape(C, 1), "br": f["br"].reshape(1, 1),
        "f_w1": f["w1"], "f_b1": columns(f["b1"]),
        "f_w2": columns(f["w2"].T).transpose(0, 2, 1), "f_b2": f["b2"].reshape(1, C),
    }
    shapes = {"conv_w": m["conv_w"], "A_log": m["A_log"], "dt_proj_w": m["dt_proj_w"]}

    nc = _bacc.Bacc("TRN2", target_bir_lowering=False, num_devices=1)
    arrays, args = {}, {}
    for name, v in laid.items():
        v = np.ascontiguousarray(v)
        arrays[f"in_{name}"] = v
        args[name] = nc.dram_tensor(f"in_{name}", v.shape, _mybir.dt.from_np(v.dtype), kind="ExternalInput").ap()
    args.update(shapes)
    out = nc.dram_tensor("out", (B, C, H * W), _mybir.dt.float32, kind="ExternalOutput").ap()
    conv_attn_mamba_mod_kernel(nc, args, out)
    r = _run(nc, [arrays], core_ids=[0])
    return r.results[0]["out"].reshape(B, C, H, W)
```

```python
import concourse.bass as bass
from concourse import mybir
from contextlib import ExitStack
import numpy as np

def conv_attn_mamba_mod_kernel(nc, I, out):
    fp32 = mybir.dt.float32
    bf16 = mybir.dt.bfloat16
    ALU = mybir.AluOpType
    ACT = mybir.ActivationFunctionType
    AX = mybir.AxisListType

    B, C, T = I["x"].shape
    P = 128
    NB = T // P
    BANK = 512
    NCH = T // BANK
    QB = BANK // P
    DIRS, DI, KCONV = I["conv_w"].shape
    NH = DI // P
    DS = I["A_log"].shape[2]
    DR = I["dt_proj_w"].shape[2]
    HM = I["w1"].shape[1] // P
    HF = I["f_w1"].shape[1] // P
    PAD = KCONV - 1
    KEPT = T // 2 - 1
    SCALE = float(np.float32(1.0) / np.sqrt(np.float32(C)))
    EPS = 1e-5
    SLOPE = 0.01
    EXP_MAX = 1e15
    STEPS = DS * NCH
    ALL = DIRS * STEPS
    QUAD = 32
    BROWS = 2 * QUAD + DS
    DT_ROWS = [QUAD * n + DS for n in range(3)] + [3 * QUAD, 3 * QUAD + DR]
    DT_PLACES = [(DT_ROWS[0], 0, 0), (DT_ROWS[1], 0, 0), (DT_ROWS[2], 0, 0), (DT_ROWS[3], 0, 1), (DT_ROWS[4], 0, 2),
                 (DT_ROWS[1], 1, 1)]
    SPLIT = 3 * QUAD
    XROWS = 3 * QUAD + 2 * DR

    LEAD_BC, LEAD_KEPT, LEAD_DBX = 3, 2, 1

    HB, BB, Z, X, Y = 0, 2, 3, 4, 6

    AT_SKIP = {1: (1, 5), 0: (65, 66)}
    STEP_GATE = {1: (2, 2, 4, 5), 0: (33, 33, 36, 39)}
    AT_M1 = (9, 14)
    AT_MSUM = (13, 16)
    STEP_MT = (7, 9)
    STEP_B2 = (10, 14)
    AT_W1 = (28, 28)
    AT_HID1 = (28, 30)
    AT_LEAKY = (31, 31)
    AT_W2 = (33, 33)
    AT_T2 = 36
    STEP_BASE = (26, 26)
    AT_W = 48
    AT_WKEEP = 50
    AT_WTURN = 50
    AT_WCOL = 51
    AT_RANK = (52, 53, 55, 56, 56, 57, 58, 59)
    AT_COUNT = (52, 54, 55, 56, 57, 58, 59, 59)
    AT_WK = 60
    AT_HID = (49, 51, 53, 54)
    AT_GELU = (52, 52, 55, 55)
    AT_FFN = (56, 57, 58, 59)
    AT_T3 = (61, 61)
    AT_OUT = 62
    AT_OUTKEEP = 63
    LN_STATS = {0: (92, 95), 1: (16, 17), 2: (37, 37)}
    LN_AGGR = {0: (95, 96), 1: (16, 19), 2: (39, 39)}
    STEP_LN = {0: 48, 1: 9, 2: 19}
    LN_APPLY = {0: (99, 99), 1: (22, 22), 2: (39, 43)}
    LN_TURN = {0: 100, 1: 24, 2: 45}
    LN_KEEP = {0: 101, 1: 26, 2: 46}
    AT_XT = 2
    AT_XTOK = 5
    AT_Q = 5
    AT_QKEEP = 8
    AT_K = 6
    AT_KKEEP = 9
    AT_V = 7
    AT_VKEEP = 10
    AT_T1OLD = 33
    AT_S = (60, 65, 68, 72, 76, 79, 84, 86)
    AT_MAX = (62, 67, 69, 74, 79, 81, 85, 87)
    AT_EXP = (63, 67, 70, 75, 78, 82, 86, 87)
    AT_RINV = (65, 69, 76, 77, 85, 86, 90, 90)
    AT_PT = (65, 69, 74, 77, 80, 83, 87, 91)
    AT_PTKEEP = (69, 71, 76, 79, 83, 86, 90, 92)
    AT_PV = (69, 75, 78, 81, 85, 87, 92, 93)
    AT_T1 = (70, 76, 79, 83, 86, 89, 93, 94)
    AT_Z = {0: (11, 11), 1: (89, 93)}
    AT_ZKEEP = {0: (14, 14), 1: (95, 95)}
    AT_YT = (63, 63)
    AT_M0 = (95, 95)
    AT_M0KEEP = 99
    AT_CONV = {1: (15, 16, 17, 19, 19, 20, 22, 22), 0: (101, 103, 103, 105, 105, 109, 110, 110)}
    AT_XC = {1: (24, 24), 0: (112, 112)}
    AT_ROWS = {1: (25, 29), 0: (111, 113)}
    AT_ROWKEEP = {1: (27, 30), 0: (114, 115)}
    AT_C = {1: 31, 0: 117}
    AT_CKEEP = {1: 34, 0: 119}
    AT_BHI = {1: 33, 0: 115}
    AT_BR1 = 117
    AT_BMID = {1: 35, 0: 117}
    AT_BR2 = 118
    AT_BLO = {1: 35, 0: 119}
    AT_DT = {1: (36, 37, 38, 40), 0: (119, 120)}
    AT_DTEXP = {1: (36, 37, 38, 39), 0: (122, 122)}
    AT_CUT = (122, 123)
    AT_LOG = {1: (41, 41), 0: (122, 123)}
    AT_DTMAX = {1: (42, 43), 0: (125, 125)}
    AT_U = (125, 125)
    STEP_BR1 = 17
    STEP_BR2 = 17
    STEP_CUT = (19, 20)
    STEP_U = (22, 28, 28, 29)

    def due(slots, g):
        return [part for part, at in enumerate(slots) if at == g]

    ctx = ExitStack()
    with ctx:
        def sb(name, shape, dtype=fp32):
            return ctx.enter_context(nc.sbuf_tensor(name, shape, dtype))

        turn_sems = []

        def sem(name):
            s = ctx.enter_context(nc.semaphore(name))
            turn_sems.append(s)
            return s

        ident = sb("ident", [P, P])
        above = sb("above", [P, P])
        pick = sb("pick", [BROWS, DS], bf16)
        ones_row = sb("ones_row", [1, P])
        ones_col = sb("ones_col", [P, 1], bf16)
        wq = sb("wq", [C, C])
        wk = sb("wk", [C, C])
        wv = sb("wv", [C, C])
        bq = sb("bq", [C, 1])
        bk = sb("bk", [C, 1])
        bv_rows = sb("bv_rows", [P, C])
        w_z = sb("w_z", [C, DIRS, DI])
        w_conv = sb("w_conv", [C, DIRS, KCONV, DI])
        conv_b = sb("conv_b", [P, DIRS, NH])
        w_rows = sb("w_rows", [P, DIRS, NH, XROWS])
        w_c = sb("w_c", [P, DIRS, NH, DS])
        w_dt = sb("w_dt", [XROWS, 2, DIRS, DI], bf16)
        b_dt = sb("b_dt", [P, DIRS, NH])
        a_neg = sb("a_neg", [P, DIRS, NH, DS])
        d_skip = sb("d_skip", [P, DIRS, NH])
        w_out = sb("w_out", [P, DIRS, NH, C])
        ln_g = sb("ln_g", [C, 1])
        ln_b = sb("ln_b", [C, 1])
        w1 = sb("w1", [C, HM * P])
        b1 = sb("b1", [P, HM])
        w2 = sb("w2", [P, HM, C])
        b2_rows = sb("b2_rows", [P, C])
        wr = sb("wr", [C, 1])
        wr_cols = sb("wr_cols", [C, P])
        br = sb("br", [P, 1])
        f_w1 = sb("f_w1", [C, HF * P])
        f_b1 = sb("f_b1", [P, HF])
        f_w2 = sb("f_w2", [P, HF, C])
        f_b2 = sb("f_b2", [1, C])
        minus_half = sb("minus_half", [P, NB])

        q = sb("q", [C, T])
        k = sb("k", [C, T])
        v_tok = sb("v_tok", [P, NB, C])
        x_tok = sb("x_tok", [P, NB, C])
        nmax = sb("nmax", [P, NB])
        rowsum = sb("rowsum", [P, NB])
        rinv = sb("rinv", [P, NB])
        t1 = sb("t1", [P, NB, C])
        t1_old = sb("t1_old", [P, NB, C])
        stats = sb("stats", [P, NB, 6])
        mean_var = sb("mean_var", [P, NB, 2])
        var_eps = sb("var_eps", [P, NB])
        rstd = sb("rstd", [P, NB])
        shift = sb("shift", [P, NB])
        x_pad = sb("x_pad", [C, PAD + T + PAD])
        xc = sb("xc", [P, DIRS, NH, T])
        dt = sb("dt", [P, DIRS, NH, T])
        u = sb("u", [P, DIRS, NH, T])
        sz = sb("sz", [P, NH, T])
        rows = sb("rows", [XROWS, T])
        b_parts = sb("b_parts", [XROWS, DIRS, T], bf16)
        c_tok = sb("c_tok", [P, DIRS, NB, DS])
        b_all = sb("b_all", [P, 2, BANK])
        dbx = sb("dbx", [P, 2, NH, BANK])
        da = sb("da", [P, 2, NH, T])
        h = sb("h", [P, 2, NH, BANK])
        y_tok = sb("y_tok", [P, NB, DI])
        m0 = sb("m0", [P, NB, C])
        res = sb("res", [P, NB, C])
        tile_a = sb("tile_a", [P, T])
        tile_b = sb("tile_b", [P, T])
        tile_c = sb("tile_c", [P, T])
        hid = sb("hid", [P, HF, T])
        heavier = sb("heavier", [P, 2, T], bf16)
        ties = sb("ties", [P, 2, P], bf16)
        w_col = sb("w_col", [P, NB])
        w_kept = sb("w_kept", [P, NB])

        def by_block(tile):
            return tile.rearrange("p (b c) -> p b c", c=C)

        m, n2, probs_t = by_block(tile_a[:, :]), by_block(tile_a[:, :]), by_block(tile_a[:, :])
        m_normed, n2c, out_s = by_block(tile_b[:, :]), tile_b[:, :], tile_b[:, :]
        x_in, w_row, probs = tile_c[:, :], tile_c[:, :], tile_c[:, :]
        h1 = hid[:, HM, :]
        in_cols = hid[:, 0:DIRS * DI // T + 1, :].rearrange("p a t -> p (a t)")[:, 0:DIRS * DI].rearrange(
            "p (r e) -> p r e", r=DIRS)
        dt_weight = tile_a[0:DR, 0:DIRS * DI].rearrange("p (r e) -> p r e", r=DIRS)
        dt_parts = heavier[0:DR].rearrange("p a t -> p (a t)")[:, 0:3 * DIRS * DI].rearrange(
            "p (n r e) -> p n r e", n=3, r=DIRS)
        ln_tile = {0: (t1, x_tok), 1: (m, m_normed), 2: (res, n2)}

        ps = ctx.enter_context(nc.psum_tensor("ps", [P, 8, BANK], fp32))

        def banks(n):
            return ps[:, n:n + 2, :].rearrange("p b c -> p (b c)")

        def blocks(n):
            return by_block(banks(n))

        def cols(c):
            return slice(c * BANK, (c + 1) * BANK)

        loaded = ctx.enter_context(nc.semaphore("loaded"))
        zeroed = ctx.enter_context(nc.semaphore("zeroed"))
        picked = ctx.enter_context(nc.semaphore("picked"))
        setup_exp = ctx.enter_context(nc.semaphore("setup_exp"))
        dt_split = ctx.enter_context(nc.semaphore("dt_split"))
        placed = ctx.enter_context(nc.semaphore("placed"))

        with nc.Block() as block:
            loads = [
                (wq[:], I["wq"]), (wk[:], I["wk"]), (wv[:], I["wv"]),
                (bq[:], I["bq"]), (bk[:], I["bk"]),
                (bv_rows[:], I["bv"].to_broadcast([P, C])),
                (in_cols, I["in_proj"][:, :, 0:DI].rearrange("r c e -> c r e")),
                (w_z[:], I["in_proj"][:, :, DI:2 * DI].rearrange("r c e -> c r e")),
                (w_conv[:].rearrange("p r k e -> p (r k e)"), I["conv_rows"].to_broadcast([P, DIRS * KCONV * DI])),
                (conv_b[:], I["conv_b"]),
                (w_c[:], I["x_proj"][:, :, :, DR + DS:DR + 2 * DS]),
                (dt_weight, I["dt_w"]), (b_dt[:], I["dt_b"]),
                (a_neg[:], I["A_logs"]), (d_skip[:], I["Dp"]), (w_out[:], I["out_w"]),
                (ln_g[:], I["ln_g"]), (ln_b[:], I["ln_b"]),
                (w1[:], I["w1"]), (b1[:], I["b1"]), (w2[:], I["w2"]), (b2_rows[:], I["b2"].to_broadcast([P, C])),
                (wr[:], I["wr"]), (br[:], I["br"].to_broadcast([P, 1])),
                (f_w1[:], I["f_w1"]), (f_b1[:], I["f_b1"]), (f_w2[:], I["f_w2"]), (f_b2[:], I["f_b2"]),
            ]
            row_loads = [(slice(QUAD * n, QUAD * n + DS), slice(DR, DR + DS)) for n in range(3)]
            row_loads += [(slice(at, at + DR), slice(0, DR)) for at in DT_ROWS]
            n_loads = len(loads) + len(row_loads)

            @block.sync
            def _(sp):
                with nc.allow_non_contiguous_dma(reason="weights, once"):
                    for dst, src in loads:
                        sp.dma_start(dst, src).then_inc(loaded, 16)
                    for dst, src in row_loads:
                        sp.dma_start(w_rows[:, :, :, dst], I["x_proj"][:, :, :, src]).then_inc(loaded, 16)
                sp.wait_ge(zeroed, 1)
                sp.wait_ge(dt_split, 5)
                for at, product, part in DT_PLACES:
                    sp.dma_start(w_dt[at:at + DR, product], dt_parts[:, part]).then_inc(placed, 16)
                sp.wait_ge(placed, 16 * len(DT_PLACES))
                sp.wait_ge(loaded, 16 * n_loads)

            @block.gpsimd
            def _(pool):
                pool.memset(w_dt[:], 0.0).then_inc(zeroed, 1)
                pool.memset(ident[:], 0.0).then_inc(zeroed, 1)
                pool.memset(above[:], 1.0).then_inc(zeroed, 1)
                pool.memset(pick[:], 0.0).then_inc(zeroed, 1)
                pool.memset(ones_row[:], 1.0)
                pool.memset(minus_half[:], -0.5)
                pool.memset(ones_col[:], 1.0)
                pool.memset(x_pad[:], 0.0)
                pool.wait_ge(zeroed, 4)
                pool.affine_select(out=ident[:], in_=ident[:], compare_op=ALU.not_equal, fill=1.0,
                                   base=0, pattern=[[-1, P]], channel_multiplier=1)
                pool.affine_select(out=above[:], in_=above[:], compare_op=ALU.is_gt, fill=0.0,
                                   base=0, pattern=[[1, P]], channel_multiplier=-1)
                for n in range(3):
                    if n:
                        pool.wait_ge(picked, n)
                    pool.affine_select(out=pick[:], in_=pick[:], compare_op=ALU.not_equal, fill=1.0,
                                       base=-QUAD * n, pattern=[[-1, DS]], channel_multiplier=1).then_inc(picked, 1)

            @block.scalar
            def _(act):
                act.wait_ge(loaded, 16 * n_loads)
                act.activation(a_neg[:], a_neg[:], ACT.Exp).then_inc(setup_exp, 1)

            @block.vector
            def _(dve):
                dve.wait_ge(loaded, 16 * n_loads)
                dve.tensor_scalar(bq[:], bq[:], SCALE, None, ALU.mult)
                dve.tensor_copy(wr_cols[:], wr[:].to_broadcast([C, P]))
                for r in range(DIRS):
                    for tap in range(KCONV):
                        dve.tensor_tensor(w_conv[:, r, tap, :], w_conv[:, r, tap, :], in_cols[:, r, :], ALU.mult)
                for part in range(3):
                    if part:
                        dve.wait_ge(dt_split, 2 * part - 1)
                        dve.tensor_tensor(dt_weight, dt_weight, dt_parts[:, part - 1], ALU.subtract
                                          ).then_inc(dt_split, 1)
                        dve.wait_ge(dt_split, 2 * part)
                    dve.tensor_copy(dt_parts[:, part], dt_weight).then_inc(dt_split, 1)
                dve.wait_ge(setup_exp, 1)
                dve.tensor_scalar(a_neg[:], a_neg[:], -1.0, None, ALU.mult)

        x_loaded, stored = sem("x_loaded"), sem("stored")
        xt_made, xt_kept = sem("xt_made"), sem("xt_kept")
        q_made, k_made, v_made = sem("q_made"), sem("k_made"), sem("v_made")
        q_kept, k_kept, v_kept = sem("q_kept"), sem("k_kept"), sem("v_kept")
        scores_made, max_made, probs_made = sem("scores_made"), sem("max_made"), sem("probs_made")
        probs_turned, probs_kept = sem("probs_turned"), sem("probs_kept")
        attn_made, rinv_made, t1_made = sem("attn_made"), sem("rinv_made"), sem("t1_made")
        t1_moved = sem("t1_moved")
        ln_stats = [sem(f"ln_stats{n}") for n in range(3)]
        ln_var = [sem(f"ln_var{n}") for n in range(3)]
        ln_eps = [sem(f"ln_eps{n}") for n in range(3)]
        ln_rstd = [sem(f"ln_rstd{n}") for n in range(3)]
        ln_made = [sem(f"ln_made{n}") for n in range(3)]
        ln_turned = [sem(f"ln_turned{n}") for n in range(3)]
        ln_kept = [sem(f"ln_kept{n}") for n in range(3)]

        def two(name):
            return [sem(f"{name}{r}") for r in range(DIRS)]

        xc_made, xc_kept = two("xc_made"), two("xc_kept")
        z_made, z_kept = two("z_made"), two("z_kept")
        rows_made, rows_kept = two("rows_made"), two("rows_kept")
        c_made, c_kept = two("c_made"), two("c_kept")
        b_high, b_mid, b_low = two("b_high"), two("b_mid"), two("b_low")
        b_rest1, b_rest2 = two("b_rest1"), two("b_rest2")
        dt_made, dt_in, dt_exp, dt_log = two("dt_made"), two("dt_in"), two("dt_exp"), two("dt_log")
        dt_cut, dt_kept = two("dt_cut"), two("dt_kept")
        u_made = two("u_made")
        y_turned, y_skip, y_gated = two("y_turned"), two("y_skip"), two("y_gated")
        b_cast, b_cast_kept = sem("b_cast"), sem("b_cast_kept")
        dbx_made, da_made = sem("dbx_made"), sem("da_made")
        h_made, h_turned, y_added = sem("h_made"), sem("h_turned"), sem("y_added")
        m0_made, m0_kept = sem("m0_made"), sem("m0_kept")
        m1_made, m_kept = sem("m1_made"), sem("m_kept")
        hid1_made, hid1_kept, hid1_leaky = sem("hid1_made"), sem("hid1_kept"), sem("hid1_leaky")
        mlp_made, mt_made, b2_added = sem("mlp_made"), sem("mt_made"), sem("b2_added")
        t2_made, base_made = sem("t2_made"), sem("base_made")
        w_made, w_row_kept, w_turned, w_col_kept = (sem(n) for n in ("w_made", "w_row_kept", "w_turned", "w_col_kept"))
        compared, counted, w_kept_made = sem("compared"), sem("counted"), sem("w_kept_made")
        hid2_made, hid2_kept, ffn_made, t3_made = (sem(n) for n in ("hid2_made", "hid2_kept", "ffn_made", "t3_made"))
        out_turned, out_kept = sem("out_turned"), sem("out_kept")

        def rest(r):
            return rows[0:SPLIT, :], rows[0:SPLIT, :], b_parts[0:SPLIT, r, :]

        def turn(image, last, now, nxt):

            first_cast = LEAD_BC if now else ALL
            first_kept = LEAD_KEPT if now else ALL
            first_dbx = LEAD_DBX + 1 if now else ALL
            first_da = 1 if now else DIRS * DS
            end_step = ALL if now else 0

            def made_ahead(n):
                return n < ALL or nxt

            with nc.Block() as block:

                @block.sync
                def _(sp):
                    if nxt:
                        sp.dma_start(x_in, I["x"][image + 1]).then_inc(x_loaded, 16)
                    if last:
                        sp.wait_ge(out_kept, 1)
                        sp.dma_start(out[image - 1], out_s).then_inc(stored, 16)
                        sp.wait_ge(stored, 16)

                @block.tensor
                def _(pe):
                    def mm(o, a, b, first=True, last=True):
                        return nc.tensor.matmul(o, a, b, start=first, stop=last)

                    def flip(o, src):
                        return nc.tensor.transpose(o, src, ident[:])

                    def turn_h(n, part):
                        if part == 0:
                            pe.wait_ge(h_made, NH * (n + 1))
                        if n:
                            pe.wait_ge(y_added, QB * (n - 1) + 2 * (part + 1))
                        for b in range(2):
                            for half in range(NH):
                                t = flip(ps[:, HB + part, (NH * b + half) * P:(NH * b + half + 1) * P],
                                         h[:, n % 2, half, (2 * part + b) * P:(2 * part + b + 1) * P])
                        t.then_inc(h_turned, 1)

                    def cast_b(n):
                        r, (s, c) = n // STEPS % DIRS, divmod(n % STEPS, NCH)
                        if n % STEPS == 0:
                            pe.wait_ge(b_low[r], 1)
                        if n > first_cast or now:
                            pe.wait_ge(b_cast_kept, n - first_kept)
                        mm(ps[:, BB, :], pick[:, s:s + 1].to_broadcast([BROWS, P]), b_parts[0:BROWS, r, cols(c)]
                           ).then_inc(b_cast, 1)

                    def tokens(r, tap, c):
                        if r == 0:
                            return x_pad[:, tap + c * BANK:tap + (c + 1) * BANK]
                        at = T + 2 * PAD - 1 - tap - c * BANK
                        return x_pad[:, at:at - BANK:-1]

                    def conv(r, part):
                        half, c, pair = part // (2 * NCH), part // 2 % NCH, part % 2
                        bank = (X, Y)[half] + c
                        for tap in (2 * pair, 2 * pair + 1):
                            t = mm(ps[:, bank, :], w_conv[:, r, tap, half * P:(half + 1) * P], tokens(r, tap, c),
                                   tap == 0, tap == KCONV - 1)
                        if c == NCH - 1 and pair == 1:
                            t.then_inc(xc_made[r], 1)

                    def gate(r, half, bank):
                        for c in range(NCH):
                            t = mm(ps[:, bank + c, :], w_z[:, r, half * P:(half + 1) * P], tokens(r, PAD, c))
                        t.then_inc(z_made[r], 1)

                    def turn_y(r, half):
                        for i in range(NB):
                            t = flip(banks((X, Y)[half])[:, i * P:(i + 1) * P], y_tok[:, i, half * P:(half + 1) * P])
                        t.then_inc(y_turned[r], 1)

                    def project(r, part, bank, made):
                        for b in range(QB):
                            i = QB * part + b
                            for half in range(NH):
                                t = mm(ps[:, bank, b * C:(b + 1) * C], xc[:, r, half, i * P:(i + 1) * P],
                                       w_out[:, r, half, :], half == 0, half == NH - 1)
                        t.then_inc(made, 1)

                    def turn_blocks(src, bank):
                        for i in range(NB):
                            t = flip(banks(bank)[:, i * P:(i + 1) * P], src[:, i, :])
                        return t

                    def before_scan(g, r):
                        for part in due(AT_CONV[r], g):
                            if part == 0 and r == 1:
                                pe.wait_ge(z_kept[0], NH)
                            if part == 0 and r == 0:
                                pe.wait_ge(ln_kept[0], 1)
                                if now:
                                    pe.wait_ge(m0_kept, 1)
                            conv(r, part)
                        for c in due(AT_ROWS[r], g):
                            if c == 0:
                                pe.wait_ge(xc_kept[r], NH)
                                if r == 1 and last:
                                    pe.wait_ge(m_kept, 2)
                                if r == 0:
                                    pe.wait_ge(t1_made, NB)
                            else:
                                pe.wait_ge(rows_kept[r], c)
                            for half in range(NH):
                                t = mm(ps[0:XROWS, Z, :], w_rows[:, r, half, :], xc[:, r, half, cols(c)],
                                       half == 0, half == NH - 1)
                            t.then_inc(rows_made[r], 1)
                        if g == AT_C[r]:
                            pe.wait_ge(rows_kept[r], NCH)
                            for i in range(NB):
                                for half in range(NH):
                                    t = mm(ps[:, Z, i * DS:(i + 1) * DS], xc[:, r, half, i * P:(i + 1) * P],
                                           w_c[:, r, half, :], half == 0, half == NH - 1)
                            t.then_inc(c_made[r], 1)
                        for part in due(AT_DT[r], g):
                            pe.wait_ge(b_low[r], 1)
                            if r:
                                half, some = part // NCH, (part % NCH,)
                                if part == 0:
                                    pe.wait_ge(c_kept[1], 1)
                                else:
                                    pe.wait_ge(dt_exp[1], part)
                            else:
                                half, some = part, range(NCH)
                            for c in some:
                                bank = Z if r else (X, Y)[half] + c
                                mm(ps[:, bank, :], w_dt[:, 0, r, half * P:(half + 1) * P], b_parts[:, r, cols(c)],
                                   True, False)
                                t = mm(ps[:, bank, :], w_dt[0:2 * QUAD, 1, r, half * P:(half + 1) * P],
                                       b_parts[0:2 * QUAD, r, cols(c)], False, True)
                            t.then_inc(dt_made[r], 1)

                    def finish_last(g):
                        for part in due(AT_M1, g):
                            pe.wait_ge(y_gated[1], NH * (part + 1))
                            if part:
                                pe.wait_ge(m_kept, part)
                            project(1, part, Z, m1_made)
                        if g == LN_TURN[1]:
                            pe.wait_ge(ln_made[1], NB)
                            if now:
                                pe.wait_ge(xc_kept[1], NH)
                            turn_blocks(m_normed, X).then_inc(ln_turned[1], 1)
                        for o in due(AT_W1, g):
                            pe.wait_ge(ln_kept[1], 1)
                            for c in range(NCH):
                                t = mm(ps[:, (Y, X)[o] + c, :], w1[:, o * P:(o + 1) * P], h1[:, cols(c)])
                            t.then_inc(hid1_made, 1)
                        for part in due(AT_W2, g):
                            pe.wait_ge(hid1_leaky, HM)
                            for b in range(QB):
                                i = QB * part + b
                                for o in range(HM):
                                    t = mm(ps[:, Y + part, b * C:(b + 1) * C], hid[:, o, i * P:(i + 1) * P], w2[:, o, :],
                                           o == 0, o == HM - 1)
                            t.then_inc(mlp_made, 1)
                        if g == LN_TURN[2]:
                            pe.wait_ge(ln_made[2], NB)
                            turn_blocks(n2, X).then_inc(ln_turned[2], 1)
                        if g == AT_W:
                            pe.wait_ge(ln_kept[2], 1)
                            for c in range(NCH):
                                t = mm(ps[:, Y + c, :], wr_cols[:], n2c[:, cols(c)])
                            t.then_inc(w_made, 1)
                        for o in due(AT_HID, g):
                            if o == 1:
                                pe.wait_ge(w_row_kept, 1)
                            if o >= 2:
                                pe.wait_ge(hid2_kept, o - 1)
                            for c in range(NCH):
                                t = mm(ps[:, (X, Y)[o % 2] + c, :], f_w1[:, o * P:(o + 1) * P], n2c[:, cols(c)])
                            t.then_inc(hid2_made, 1)
                        if g == AT_WTURN:
                            pe.wait_ge(w_row_kept, 1)
                            if now:
                                pe.wait_ge(dt_exp[1], NH * NCH)
                            for i in range(NB):
                                t = nc.tensor.transpose(ps[:, Z, i:i + 1], w_row[0:1, i * P:(i + 1) * P],
                                                        ident[0:1, 0:1])
                            t.then_inc(w_turned, 1)
                        for j in due(AT_COUNT, g):
                            pe.wait_ge(compared, min(3 * (j + 1), 3 * NB - 1))
                            for i in range(NB):
                                mm(ps[:, Z, i:i + 1], heavier[:, j % 2, i * P:(i + 1) * P], ones_col[:],
                                   j == 0 and i == 0, False)
                            mm(ps[:, Z, j:j + 1], ties[:, j % 2, :], ones_col[:], False, j == NB - 1
                               ).then_inc(counted, 1)
                        for pair in due(AT_FFN, g):
                            if pair == 0:
                                pe.wait_ge(hid2_kept, HF)
                            for i in (2 * pair, 2 * pair + 1):
                                for o in range(HF):
                                    mm(banks(X)[:, i * C:(i + 1) * C], hid[:, o, i * P:(i + 1) * P], f_w2[:, o, :],
                                       o == 0, False)
                                t = mm(banks(X)[:, i * C:(i + 1) * C], ones_row[:], f_b2[:], False, True)
                            t.then_inc(ffn_made, 1)
                        if g == AT_OUT:
                            pe.wait_ge(t3_made, NB)
                            turn_blocks(res, Y).then_inc(out_turned, 1)

                    def attend_next(g):
                        if g == AT_XT:
                            pe.wait_ge(x_loaded, 16)
                            if last:
                                pe.wait_ge(y_skip[1], 1)
                            for i in range(NB):
                                t = flip(banks(X)[:, i * C:(i + 1) * C], x_in[:, i * P:(i + 1) * P])
                            t.then_inc(xt_made, 1)
                        for at, w, bank, made in ((AT_Q, wq, Y, q_made), (AT_K, wk, X, k_made)):
                            if g == at:
                                if g == AT_Q and last:
                                    pe.wait_ge(y_skip[1], 2)
                                if g == AT_K:
                                    pe.wait_ge(xt_kept, 1)
                                for c in range(NCH):
                                    t = mm(ps[:, bank + c, :], w[:], x_in[:, cols(c)])
                                t.then_inc(made, 1)
                        if g == AT_V:
                            pe.wait_ge(q_kept, 1)
                            for i in range(NB):
                                t = mm(banks(Y)[:, i * C:(i + 1) * C], x_in[:, i * P:(i + 1) * P], wv[:])
                            t.then_inc(v_made, 1)
                        for i in due(AT_S, g):
                            if i == 0:
                                pe.wait_ge(k_kept, 1)
                                if last:
                                    pe.wait_ge(t3_made, NB)
                            else:
                                pe.wait_ge(probs_made, i)
                                if now and i == 1:
                                    pe.wait_ge(y_skip[0], 1)
                            for c in range(NCH):
                                t = mm(ps[:, X + c, :], q[:, i * P:(i + 1) * P], k[:, cols(c)])
                            t.then_inc(scores_made, 1)
                        for i in due(AT_PT, g):
                            pe.wait_ge(probs_made, i + 1)
                            if i == 0:
                                pe.wait_ge(v_kept, 1)
                                if now:
                                    pe.wait_ge(y_skip[0], 2)
                            else:
                                pe.wait_ge(probs_kept, i)
                            for b in range(NB):
                                t = flip(banks(Y)[:, b * P:(b + 1) * P], probs[:, b * P:(b + 1) * P])
                            t.then_inc(probs_turned, 1)
                        for i in due(AT_PV, g):
                            pe.wait_ge(probs_kept, i + 1)
                            if i == 0 and last:
                                pe.wait_ge(w_kept_made, 1)
                            elif i == 0 and now:
                                pe.wait_ge(dt_exp[1], NH * NCH)
                            if i:
                                pe.wait_ge(t1_made, i)
                            for b in range(NB):
                                t = mm(ps[:, Z, 0:C], probs_t[:, b, :], v_tok[:, b, :], b == 0, b == NB - 1)
                            t.then_inc(attn_made, 1)
                        if g == LN_TURN[0]:
                            pe.wait_ge(ln_made[0], NB)
                            pe.wait_ge(probs_kept, NB)
                            if now:
                                pe.wait_ge(z_kept[1], NH)
                            turn_blocks(x_tok, Y).then_inc(ln_turned[0], 1)

                    def aside(g):
                        if last:
                            finish_last(g)
                        if nxt:
                            attend_next(g)
                            before_scan(g, 0)
                        if now:
                            before_scan(g, 1)
                            for half in due(AT_YT, g):
                                pe.wait_ge(y_added, QB * STEPS)
                                if nxt and half == 0:
                                    pe.wait_ge(probs_made, 1)
                                if last and half == 1:
                                    pe.wait_ge(out_kept, 1)
                                turn_y(0, half)
                            for r in range(DIRS):
                                for half in due(AT_Z[r], g):
                                    if r == 0:
                                        if last:
                                            pe.wait_ge(y_skip[1], half + 1)
                                        if nxt:
                                            pe.wait_ge((k_kept, v_kept)[half], 1)
                                    elif nxt:
                                        pe.wait_ge((probs_made, probs_kept)[half], NB)
                                    else:
                                        pe.wait_ge(y_skip[0], half + 1)
                                    gate(r, half, (X, Y)[half])
                            for part in due(AT_M0, g):
                                pe.wait_ge(z_kept[1], NH)
                                pe.wait_ge(y_gated[0], NH * NCH)
                                project(0, part, X + part, m0_made)

                    if last:
                        for half in range(NH):
                            turn_y(1, half)
                    for n in range(end_step):
                        turn_h(n, 0)
                        aside(2 * n)
                        turn_h(n, 1)
                        if made_ahead(n + LEAD_BC):
                            cast_b(n + LEAD_BC)
                        aside(2 * n + 1)
                    if not now:
                        for g in range(2 * ALL):
                            aside(g)
                        if nxt:
                            for n in range(LEAD_BC):
                                cast_b(ALL + n)

                @block.scalar
                def _(act):
                    def decay(n):
                        s, half = divmod(n, NH)
                        r = s // DS % DIRS
                        if s % DS == 0:
                            act.wait_ge(dt_kept[r], half + 1)
                        if now and s >= 2:
                            act.wait_ge(h_made, NH * (NCH * (s - 1) - 1) + half + 1)
                        act.activation(da[:, s % 2, half, :], dt[:, r, half, :], ACT.Exp,
                                       scale=a_neg[:, r, half, s % DS:s % DS + 1]).then_inc(da_made, 1)

                    def keep_b(n):
                        if n >= first_cast:
                            act.wait_ge(b_cast, n - first_cast + 1)
                        if n - 2 >= first_dbx:
                            act.wait_ge(dbx_made, n - 2 - first_dbx + 1)
                        act.activation(b_all[:, n % 2, :], ps[:, BB, :], ACT.Copy).then_inc(b_cast_kept, 1)

                    def normalize(g, n):
                        src, dst = ln_tile[n]
                        for part in due(LN_APPLY[n], g):
                            act.wait_ge(ln_rstd[n], 1)
                            if n == 2:
                                act.wait_ge(mt_made, 2)
                            for i in range(QB * part, QB * (part + 1)):
                                act.activation(dst[:, i, :], src[:, i, :], ACT.Identity, bias=shift[:, i:i + 1],
                                               scale=rstd[:, i:i + 1]).then_inc(ln_made[n], 1)

                    def before_scan(g, r):
                        for half in due(AT_XC[r], g):
                            if r == 1 and last:
                                act.wait_ge(m1_made, 2)
                            if r == 0 and now:
                                act.wait_ge(m0_made, 2)
                            act.wait_ge(xc_made[r], half + 1)
                            act.activation(xc[:, r, half, :], banks((X, Y)[half]), ACT.Silu,
                                           bias=conv_b[:, r, half:half + 1]).then_inc(xc_kept[r], 1)
                        for c in due(AT_ROWKEEP[r], g):
                            act.wait_ge(rows_made[r], c + 1)
                            if r == 0 and now and c == 0:
                                act.wait_ge(b_low[1], 1)
                            act.activation(rows[:, cols(c)], ps[0:XROWS, Z, :], ACT.Copy).then_inc(rows_kept[r], 1)
                        if g == AT_BHI[r]:
                            act.wait_ge(rows_kept[r], NCH)
                            if r == 0 and now:
                                act.wait_ge(b_cast, STEPS - first_cast)
                            act.activation(b_parts[:, r, :], rows[:], ACT.Copy).then_inc(b_high[r], 1)
                        if g == AT_BMID[r]:
                            act.wait_ge(b_rest1[r], 1)
                            act.activation(b_parts[QUAD:2 * QUAD, r, :], rows[QUAD:2 * QUAD, :], ACT.Copy
                                           ).then_inc(b_mid[r], 1)
                            act.activation(b_parts[2 * QUAD:SPLIT, r, :], rows[2 * QUAD:SPLIT, :], ACT.Copy
                                           ).then_inc(b_mid[r], 1)
                        if g == AT_BLO[r]:
                            act.wait_ge(b_rest2[r], 1)
                            act.activation(b_parts[2 * QUAD:SPLIT, r, :], rows[2 * QUAD:SPLIT, :], ACT.Copy
                                           ).then_inc(b_low[r], 1)
                        if g == AT_CKEEP[r]:
                            act.wait_ge(c_made[r], 1)
                            if r == 0 and now:
                                act.wait_ge(y_added, QB * STEPS)
                            act.activation(c_tok[:, r, :, :].rearrange("p b s -> p (b s)"), ps[:, Z, 0:NB * DS], ACT.Copy
                                           ).then_inc(c_kept[r], 1)
                        for part in due(AT_DTEXP[r], g):
                            act.wait_ge(dt_made[r], part + 1)
                            if r:
                                half, some, src = part // NCH, cols(part % NCH), ps[:, Z, :]
                            else:
                                half, some, src = part, slice(0, T), banks((X, Y)[part])
                            if r == 0 and now and half == 0:
                                act.wait_ge(dbx_made, STEPS - first_dbx)
                            act.activation(dt[:, r, half, some], src, ACT.Identity, bias=b_dt[:, r, half:half + 1]
                                           ).then_inc(dt_in[r], 1)
                            act.activation(u[:, r, half, some], src, ACT.Exp, bias=b_dt[:, r, half:half + 1]
                                           ).then_inc(dt_exp[r], 1)
                        for half in due(AT_LOG[r], g):
                            act.wait_ge(dt_cut[r], half + 1)
                            act.activation(u[:, r, half, :], u[:, r, half, :], ACT.Ln, bias=1.0).then_inc(dt_log[r], 1)

                    def finish_last(g):
                        if g == LN_KEEP[1]:
                            act.wait_ge(ln_turned[1], 1)
                            act.activation(h1, banks(X), ACT.Identity, bias=ln_b[:], scale=ln_g[:]
                                           ).then_inc(ln_kept[1], 1)
                        for o in due(AT_HID1, g):
                            act.wait_ge(hid1_made, o + 1)
                            act.activation(hid[:, o, :], banks((Y, X)[o]), ACT.Identity,
                                           bias=b1[:, o:o + 1]).then_inc(hid1_kept, 1)
                        if g == LN_KEEP[2]:
                            act.wait_ge(ln_turned[2], 1)
                            act.activation(n2c, banks(X), ACT.Copy).then_inc(ln_kept[2], 1)
                        if g == AT_WKEEP:
                            act.wait_ge(w_made, 1)
                            if nxt:
                                act.wait_ge(v_made, 1)
                            act.activation(w_row, banks(Y), ACT.Identity, bias=br[:]).then_inc(w_row_kept, 1)
                        normalize(g, 1)
                        normalize(g, 2)
                        for o in due(AT_GELU, g):
                            act.wait_ge(hid2_made, o + 1)
                            act.activation(hid[:, o, :], banks((X, Y)[o % 2]), ACT.Gelu_apprx_tanh,
                                           bias=f_b1[:, o:o + 1]).then_inc(hid2_kept, 1)
                        if g == AT_OUTKEEP:
                            act.wait_ge(out_turned, 1)
                            act.activation(out_s, banks(Y), ACT.Copy).then_inc(out_kept, 1)

                    def attend_next(g):
                        if g == AT_QKEEP:
                            act.wait_ge(q_made, 1)
                            act.activation(q[:], banks(Y), ACT.Identity, bias=bq[:], scale=SCALE).then_inc(q_kept, 1)
                        if g == AT_KKEEP:
                            act.wait_ge(k_made, 1)
                            act.activation(k[:], banks(X), ACT.Identity, bias=bk[:]).then_inc(k_kept, 1)
                        if g == AT_VKEEP:
                            act.wait_ge(v_made, 1)
                            act.activation(v_tok[:], blocks(Y), ACT.Copy).then_inc(v_kept, 1)
                        for i in due(AT_EXP, g):
                            act.wait_ge(max_made, i + 1)
                            if i == 0 and last:
                                act.wait_ge(compared, 3 * NB - 1)
                                act.wait_ge(w_turned, 1)
                            if i:
                                act.wait_ge(probs_turned, i)
                            act.activation(probs, banks(X), ACT.Exp, bias=nmax[:, i:i + 1],
                                           accum_out=rowsum[:, i:i + 1]).then_inc(probs_made, 1)
                        for i in due(AT_PTKEEP, g):
                            act.wait_ge(probs_turned, i + 1)
                            if i:
                                act.wait_ge(attn_made, i)
                            elif last:
                                act.wait_ge(base_made, 2)
                            act.activation(probs_t, blocks(Y), ACT.Copy).then_inc(probs_kept, 1)
                        normalize(g, 0)
                        if g == LN_KEEP[0]:
                            act.wait_ge(ln_turned[0], 1)
                            act.activation(x_pad[:, PAD:PAD + T], banks(Y), ACT.Copy).then_inc(ln_kept[0], 1)

                    def aside(g):
                        if last:
                            finish_last(g)
                        if nxt:
                            attend_next(g)
                            before_scan(g, 0)
                        if now:
                            before_scan(g, 1)
                            for r in range(DIRS):
                                for half in due(AT_ZKEEP[r], g):
                                    if last or r == 1:
                                        act.wait_ge(y_gated[1 - r], NH * NCH)
                                    act.wait_ge(z_made[r], half + 1)
                                    act.activation(sz[:, half, :], banks((X, Y)[half]), ACT.Silu
                                                   ).then_inc(z_kept[r], 1)
                            if g == AT_T1OLD:
                                if last:
                                    act.wait_ge(mt_made, 2)
                                act.activation(t1_old[:], t1[:], ACT.Copy).then_inc(t1_moved, 1)
                            if g == AT_M0KEEP:
                                act.wait_ge(m0_made, 2)
                                if last:
                                    act.wait_ge(m_kept, 2)
                                act.activation(m0[:], blocks(X), ACT.Copy).then_inc(m0_kept, 1)

                    for n in range(end_step):
                        if n // NCH + 1 < DIRS * DS or nxt:
                            decay(n + NH)
                        aside(2 * n)
                        if made_ahead(n + LEAD_KEPT):
                            keep_b(n + LEAD_KEPT)
                        aside(2 * n + 1)
                    if not now:
                        for g in range(2 * ALL):
                            aside(g)
                        if nxt:
                            for half in range(NH):
                                decay(NH * DIRS * DS + half)
                            for n in range(LEAD_KEPT):
                                keep_b(ALL + n)

                @block.gpsimd
                def _(pool):
                    def times_b(n):
                        r, (s, c) = n // STEPS % DIRS, divmod(n % STEPS, NCH)
                        if s == 0 and n >= STEPS:
                            pool.wait_ge(u_made[r], NH * (c + 1) if r else NH)
                        if n >= first_kept:
                            pool.wait_ge(b_cast_kept, n - first_kept + 1)
                        if now and n >= 2:
                            pool.wait_ge(h_made, NH * (n - 1))
                        pool.tensor_tensor(dbx[:, n % 2, :, :], u[:, r, :, cols(c)],
                                           b_all[:, n % 2, :].unsqueeze(1).to_broadcast([P, NH, BANK]), ALU.mult
                                           ).then_inc(dbx_made, 1)

                    def inverse_deviation(n):
                        pool.wait_ge(ln_var[n], NB)
                        pool.tensor_scalar(var_eps[:], mean_var[:, :, 1], EPS, None, ALU.add).then_inc(ln_eps[n], 1)
                        if n == 0 and last:
                            pool.wait_ge(ln_made[2], NB)
                        pool.tensor_scalar(shift[:], mean_var[:, :, 0], -1.0, None, ALU.mult).then_inc(ln_eps[n], 1)
                        pool.wait_ge(ln_eps[n], 2)
                        pool.tensor_tensor(rstd[:], var_eps[:], minus_half[:], ALU.pow).then_inc(ln_eps[n], 1)
                        pool.wait_ge(ln_eps[n], 3)
                        pool.tensor_tensor(shift[:], shift[:], rstd[:], ALU.mult).then_inc(ln_rstd[n], 1)

                    def half_sum(o, a, b, part):
                        some = slice(QB * part, QB * (part + 1))
                        return pool.tensor_tensor(o[:, some, :], a[:, some, :], b[:, some, :], ALU.add)

                    def make_u(part):
                        c, half = divmod(part, NH)
                        pool.wait_ge(dt_kept[1], half + 1)
                        pool.tensor_tensor(u[:, 1, half, cols(c)], dt[:, 1, half, cols(c)], xc[:, 1, half, cols(c)],
                                           ALU.mult).then_inc(u_made[1], 1)

                    def make_gated(r, part):
                        c, half = divmod(part, NH)
                        pool.wait_ge(y_skip[r], half + 1)
                        pool.tensor_tensor(xc[:, r, half, cols(c)], xc[:, r, half, cols(c)], sz[:, half, cols(c)],
                                           ALU.mult).then_inc(y_gated[r], 1)

                    def aside(step):
                        if last:
                            for part in due(STEP_GATE[1], step):
                                make_gated(1, part)
                            for part in due(STEP_MT, step):
                                pool.wait_ge(m_kept, part + 1)
                                half_sum(res, m, t1_old, part).then_inc(mt_made, 1)
                            for part in due(STEP_B2, step):
                                pool.wait_ge(mt_made, part + 1)
                                some = slice(QB * part, QB * (part + 1))
                                pool.tensor_tensor(res[:, some, :], res[:, some, :],
                                                   b2_rows[:].unsqueeze(1).to_broadcast([P, QB, C]), ALU.add
                                                   ).then_inc(b2_added, 1)
                            for n in (1, 2):
                                if step == STEP_LN[n]:
                                    inverse_deviation(n)
                            for part in due(STEP_BASE, step):
                                pool.wait_ge(ln_made[2], NB)
                                half_sum(res, res, n2, part).then_inc(base_made, 1)
                        if nxt:
                            if step == STEP_LN[0]:
                                inverse_deviation(0)
                        if now:
                            if step == STEP_BR1:
                                pool.wait_ge(b_high[1], 1)
                                pool.tensor_tensor(*rest(1), ALU.subtract).then_inc(b_rest1[1], 1)
                            if step == STEP_BR2:
                                pool.wait_ge(b_mid[1], 2)
                                pool.tensor_tensor(*rest(1), ALU.subtract).then_inc(b_rest2[1], 1)
                            for half in due(STEP_CUT, step):
                                pool.wait_ge(dt_exp[1], NCH * (half + 1))
                                pool.tensor_scalar(u[:, 1, half, :], u[:, 1, half, :], EXP_MAX, None, ALU.min
                                                   ).then_inc(dt_cut[1], 1)
                            for part in due(STEP_GATE[0], step):
                                make_gated(0, part)
                            for part in due(STEP_U, step):
                                make_u(part)

                    for n in range(end_step):
                        if n and made_ahead(n + LEAD_DBX):
                            times_b(n + LEAD_DBX)
                        aside(n)
                    if now and nxt:
                        times_b(ALL + LEAD_DBX)
                    if not now:
                        for step in range(ALL):
                            aside(step)
                        if nxt:
                            for n in range(LEAD_DBX + 1):
                                times_b(ALL + n)

                @block.vector
                def _(dve):
                    def scan(n):
                        s, c = divmod(n, NCH)
                        for half in range(NH):
                            if n:
                                dve.wait_ge(h_made, NH * (n - 1) + half + 1)
                            if c == 0:
                                if s >= first_da:
                                    dve.wait_ge(da_made, NH * (s - first_da) + half + 1)
                                before = 0.0
                            else:
                                before = h[:, (n - 1) % 2, half, BANK - 1:BANK]
                            if n >= first_dbx and half == 0:
                                dve.wait_ge(dbx_made, n - first_dbx + 1)
                            dve.tensor_tensor_scan(h[:, n % 2, half, :], da[:, s % 2, half, cols(c)],
                                                   dbx[:, n % 2, half, :], before, ALU.mult, ALU.add
                                                   ).then_inc(h_made, 1)

                    def add_y(n, part):
                        r, (s, c) = n // STEPS, divmod(n % STEPS, NCH)
                        dve.wait_ge(h_turned, 2 * n + part + 1)
                        if s == 0 and c == 0 and part == 0 and (r == 1 or last):
                            dve.wait_ge(y_turned[1 - r], NH)
                        for b in (2 * part, 2 * part + 1):
                            i = QB * c + b
                            src = ps[:, HB + part, (b % 2) * DI:(b % 2 + 1) * DI]
                            weight = c_tok[:, r, i, s:s + 1]
                            if s == 0:
                                dve.tensor_scalar(y_tok[:, i, :], src, weight, None, ALU.mult).then_inc(y_added, 1)
                            else:
                                dve.wait_ge(y_added, QB * (n - NCH) + b + 1)
                                dve.scalar_tensor_tensor(y_tok[:, i, :], src, weight, y_tok[:, i, :],
                                                         ALU.mult, ALU.add).then_inc(y_added, 1)

                    def layer_norm(g, n):
                        src = ln_tile[n][0]
                        for part in due(LN_STATS[n], g):
                            if n == 0:
                                dve.wait_ge(t1_made, QB * (part + 1))
                            if n == 1:
                                dve.wait_ge(m_kept, part + 1)
                            if n == 2:
                                dve.wait_ge(t2_made, 1)
                            for i in range(QB * part, QB * (part + 1)):
                                dve.bn_stats(stats[:, i, :], src[:, i, :]).then_inc(ln_stats[n], 1)
                        for part in due(LN_AGGR[n], g):
                            if n == 0 and last:
                                dve.wait_ge(ln_rstd[2], 1)
                            for i in range(QB * part, QB * (part + 1)):
                                dve.wait_ge(ln_stats[n], i + 1)
                                dve.bn_aggr(mean_var[:, i, :], stats[:, i, :]).then_inc(ln_var[n], 1)

                    def skip(g, r):
                        for half in due(AT_SKIP[r], g):
                            dve.wait_ge(y_turned[r], half + 1)
                            dve.scalar_tensor_tensor(xc[:, r, half, :], xc[:, r, half, :], d_skip[:, r, half:half + 1],
                                                     banks((X, Y)[half]), ALU.mult, ALU.add).then_inc(y_skip[r], 1)

                    def before_scan(g):
                        if g == AT_BR1:
                            dve.wait_ge(b_high[0], 1)
                            dve.tensor_tensor(*rest(0), ALU.subtract).then_inc(b_rest1[0], 1)
                        if g == AT_BR2:
                            dve.wait_ge(b_mid[0], 2)
                            dve.tensor_tensor(*rest(0), ALU.subtract).then_inc(b_rest2[0], 1)
                        for half in due(AT_CUT, g):
                            dve.wait_ge(dt_exp[0], half + 1)
                            dve.tensor_scalar(u[:, 0, half, :], u[:, 0, half, :], EXP_MAX, None, ALU.min
                                              ).then_inc(dt_cut[0], 1)

                    def keep_dt(g, r):
                        for half in due(AT_DTMAX[r], g):
                            dve.wait_ge(dt_log[r], half + 1)
                            dve.tensor_tensor(dt[:, r, half, :], dt[:, r, half, :], u[:, r, half, :], ALU.max
                                              ).then_inc(dt_kept[r], 1)

                    def finish_last(g):
                        skip(g, 1)
                        for part in due(AT_MSUM, g):
                            some = slice(QB * part, QB * (part + 1))
                            dve.wait_ge(m1_made, part + 1)
                            dve.tensor_tensor(m[:, some, :], by_block(ps[:, Z, :]), m0[:, some, :], ALU.add
                                              ).then_inc(m_kept, 1)
                        layer_norm(g, 1)
                        for o in due(AT_LEAKY, g):
                            dve.wait_ge(hid1_kept, o + 1)
                            dve.scalar_tensor_tensor(hid[:, o, :], hid[:, o, :], SLOPE, hid[:, o, :],
                                                     ALU.mult, ALU.max).then_inc(hid1_leaky, 1)
                        if g == AT_T2:
                            dve.wait_ge(b2_added, 2)
                            dve.wait_ge(mlp_made, 2)
                            dve.tensor_tensor(res[:], blocks(Y), res[:], ALU.add).then_inc(t2_made, 1)
                        layer_norm(g, 2)
                        if g == AT_WCOL:
                            dve.wait_ge(w_turned, 1)
                            dve.tensor_copy(w_col[:], ps[:, Z, 0:NB]).then_inc(w_col_kept, 1)
                        for j in due(AT_RANK, g):
                            mine = slice(j * P, (j + 1) * P)
                            upto, after = slice(0, (j + 1) * P), slice((j + 1) * P, T)
                            if j == 0:
                                dve.wait_ge(w_col_kept, 1)
                                dve.wait_ge(w_row_kept, 1)
                            if j >= 2:
                                dve.wait_ge(counted, j - 1)
                            dve.tensor_scalar(heavier[:, j % 2, upto], w_row[:, upto], w_col[:, j:j + 1], None,
                                              ALU.is_lt).then_inc(compared, 1)
                            if j < NB - 1:
                                dve.tensor_scalar(heavier[:, j % 2, after], w_row[:, after], w_col[:, j:j + 1],
                                                  None, ALU.is_le).then_inc(compared, 1)
                            dve.scalar_tensor_tensor(ties[:, j % 2, :], w_row[:, mine], w_col[:, j:j + 1], above[:],
                                                     ALU.is_equal, ALU.mult).then_inc(compared, 1)
                        if g == AT_WK:
                            dve.wait_ge(counted, NB)
                            dve.scalar_tensor_tensor(w_kept[:], ps[:, Z, 0:NB], float(KEPT), w_col[:], ALU.is_lt, ALU.mult
                                                     ).then_inc(w_kept_made, 1)
                        for part in due(AT_T3, g):
                            if part == 0:
                                dve.wait_ge(w_kept_made, 1)
                            dve.wait_ge(base_made, part + 1)
                            dve.wait_ge(ffn_made, 2 * (part + 1))
                            for i in range(QB * part, QB * (part + 1)):
                                dve.scalar_tensor_tensor(res[:, i, :], blocks(X)[:, i, :], w_kept[:, i:i + 1],
                                                         res[:, i, :], ALU.mult, ALU.add).then_inc(t3_made, 1)

                    def attend_next(g):
                        if g == AT_XTOK:
                            dve.wait_ge(xt_made, 1)
                            dve.tensor_tensor(x_tok[:], blocks(X), bv_rows[:].unsqueeze(1).to_broadcast([P, NB, C]),
                                              ALU.add).then_inc(xt_kept, 1)
                        for i in due(AT_MAX, g):
                            dve.wait_ge(scores_made, i + 1)
                            dve.tensor_reduce(nmax[:, i:i + 1], banks(X), AX.X, ALU.max, negate=True
                                              ).then_inc(max_made, 1)
                        for i in due(AT_RINV, g):
                            dve.wait_ge(probs_made, i + 1)
                            dve.reciprocal(rinv[:, i:i + 1], rowsum[:, i:i + 1]).then_inc(rinv_made, 1)
                        for i in due(AT_T1, g):
                            if i == 0:
                                if now:
                                    dve.wait_ge(t1_moved, 1)
                                dve.wait_ge(xt_kept, 1)
                            dve.wait_ge(rinv_made, i + 1)
                            dve.wait_ge(attn_made, i + 1)
                            dve.scalar_tensor_tensor(t1[:, i, :], ps[:, Z, 0:C], rinv[:, i:i + 1], x_tok[:, i, :],
                                                     ALU.mult, ALU.add).then_inc(t1_made, 1)
                        layer_norm(g, 0)

                    def aside(g):
                        if last:
                            finish_last(g)
                        if nxt:
                            attend_next(g)
                            before_scan(g)
                            keep_dt(g, 0)
                            for half in due(AT_U, g):
                                dve.wait_ge(dt_kept[0], half + 1)
                                dve.tensor_tensor(u[:, 0, half, :], dt[:, 0, half, :], xc[:, 0, half, :], ALU.mult
                                                  ).then_inc(u_made[0], 1)
                        if now:
                            keep_dt(g, 1)
                            skip(g, 0)

                    for n in range(end_step):
                        scan(n)
                        if n:
                            add_y(n - 1, 0)
                        aside(2 * n)
                        if n:
                            add_y(n - 1, 1)
                        aside(2 * n + 1)
                    if now:
                        add_y(ALL - 1, 0)
                        add_y(ALL - 1, 1)
                    else:
                        for g in range(2 * ALL):
                            aside(g)

            nums = [s.num for s in turn_sems]
            nc.all_engine_barrier(sems_to_clear=range(min(nums), max(nums) + 1))

        turn(-1, last=False, now=False, nxt=True)
        turn(0, last=False, now=True, nxt=True)
        with nc.Fori(1, B - 1) as image:
            turn(image, last=True, now=True, nxt=True)
        turn(B - 1, last=True, now=True, nxt=False)
        turn(B, last=True, now=False, nxt=False)


def kernel(**inputs):
    import concourse.bacc as _bacc
    from concourse import mybir as _mybir
    from concourse.bass_utils import run_bass_kernel_spmd as _run

    a = {k: np.asarray(v) for k, v in inputs.items()}
    P = 128

    def columns(v):
        return np.moveaxis(v.reshape(*v.shape[:-1], v.shape[-1] // P, P), -1, 0)

    x = a["x"]
    B, C, H, W = x.shape
    m = {k.removeprefix("L1_attn_"): v for k, v in a.items() if k.startswith("L1_attn_")}
    f = {k.removeprefix("L1_ffn_"): v for k, v in a.items() if k.startswith("L1_ffn_")}
    DIRS, DI, KCONV = m["conv_w"].shape
    laid = {
        "x": x.reshape(B, C, H * W),
        "wq": a["L0_conv_Wq"].T, "wk": a["L0_conv_Wk"].T, "wv": a["L0_conv_Wv"].T,
        "bq": a["L0_conv_bq"].reshape(C, 1), "bk": a["L0_conv_bk"].reshape(C, 1),
        "bv": a["L0_conv_bv"].reshape(1, C),
        "in_proj": m["in_proj_w"].transpose(0, 2, 1),
        "conv_rows": m["conv_w"].transpose(0, 2, 1).reshape(1, -1),
        "conv_b": columns(m["conv_b"]),
        "x_proj": columns(m["x_proj_w"]).transpose(0, 1, 3, 2),
        "dt_w": m["dt_proj_w"].transpose(2, 0, 1),
        "dt_b": columns(m["dt_proj_b"]),
        "A_logs": columns(m["A_log"].transpose(0, 2, 1)).transpose(0, 1, 3, 2),
        "Dp": columns(m["Dp"]),
        "out_w": columns(m["out_proj_w"]).transpose(0, 1, 3, 2),
        "ln_g": m["ln_g"].reshape(C, 1), "ln_b": m["ln_b"].reshape(C, 1),
        "w1": m["w1"].T, "b1": columns(m["b1"]),
        "w2": columns(m["w2"]).transpose(0, 2, 1), "b2": m["b2"].reshape(1, C),
        "wr": f["wr"].reshape(C, 1), "br": f["br"].reshape(1, 1),
        "f_w1": f["w1"], "f_b1": columns(f["b1"]),
        "f_w2": columns(f["w2"].T).transpose(0, 2, 1), "f_b2": f["b2"].reshape(1, C),
    }
    shapes = {"conv_w": m["conv_w"], "A_log": m["A_log"], "dt_proj_w": m["dt_proj_w"]}

    nc = _bacc.Bacc("TRN2", target_bir_lowering=False, num_devices=1)
    arrays, args = {}, {}
    for name, v in laid.items():
        v = np.ascontiguousarray(v)
        arrays[f"in_{name}"] = v
        args[name] = nc.dram_tensor(f"in_{name}", v.shape, _mybir.dt.from_np(v.dtype), kind="ExternalInput").ap()
    args.update(shapes)
    out = nc.dram_tensor("out", (B, C, H * W), _mybir.dt.float32, kind="ExternalOutput").ap()
    conv_attn_mamba_mod_kernel(nc, args, out)
    r = _run(nc, [arrays], core_ids=[0])
    return r.results[0]["out"].reshape(B, C, H, W)
```
